# Optimizing a Trainium2 kernel written in Bass

```python
import numpy as np
import jax
import jax.numpy as jnp

def _softmax(x, axis=-1):
    return jax.nn.softmax(x, axis=axis)

def _gelu(x):
    return jax.nn.gelu(x, approximate=True)

def _silu(x):
    return jax.nn.silu(x)

def _sigmoid(x):
    return jax.nn.sigmoid(x)

def _layernorm(x, axis=-1, eps=1e-05):
    m = jnp.mean(x, axis=axis, keepdims=True)
    v = jnp.var(x, axis=axis, keepdims=True)
    return (x - m) / jnp.sqrt(v + eps)

def _scatter_add(tgt, idx, src, axis=0):
    return tgt.at[idx].add(src)

def _segment_sum(src, seg, n):
    return jax.ops.segment_sum(src, seg, n)
kernel_name = 'mk_seq_postln_d1_jaxref_r8_39c0b5'

def setup_inputs(seed: int=0):
    np.random.seed(seed)
    _w = jnp.asarray

    def _L0_attn_setup():
        import jax, jax.numpy as jnp
        import numpy as np
        from math import sqrt
        N_HEAD = 16
        W_SCALE = 0.02

        def _reference_tuple_inner(x, W_dq, W_uq, W_dkv, W_uk, W_uv, W_o):
            B, T, C = x.shape
            nh = N_HEAD
            hs = C // nh
            n_kvl = W_dkv.shape[0]
            k_eff = (W_dq.T @ W_uq.T @ W_uk).reshape(nh, hs, n_kvl)
            v_eff = jnp.transpose((W_uv.T @ W_o.T).reshape(n_kvl, nh, hs), (1, 0, 2))
            c_kv = x @ W_dkv.T
            q = x @ W_dq.T @ W_uq.T
            q = q.reshape(B, T, nh, hs)
            q_lat = jnp.einsum('bqhd,hdl->bhql', q, k_eff)
            attn = jnp.einsum('bhql,bkl->bhqk', q_lat, c_kv) / sqrt(hs)
            causal = jnp.tril(jnp.ones((T, T), dtype=bool))
            attn = jnp.where(causal[None, None], attn, -jnp.inf)
            attn = jax.nn.softmax(attn, axis=-1)
            y_lat = jnp.einsum('bhqk,bkl->bhql', attn, c_kv)
            y = jnp.einsum('bhql,hld->bqhd', y_lat, v_eff).reshape(B, T, C)
            return (y, c_kv)
        key = jax.random.key(seed)
        ks = jax.random.split(key, 7)
        B, T, C = (2, 256, 128)
        QL, KVL = (64, 64)
        return {'x': jax.random.normal(ks[0], (B, T, C), dtype=jnp.float32), 'W_dq': jax.random.normal(ks[1], (QL, C), dtype=jnp.float32) * W_SCALE, 'W_uq': jax.random.normal(ks[2], (C, QL), dtype=jnp.float32) * W_SCALE, 'W_dkv': jax.random.normal(ks[3], (KVL, C), dtype=jnp.float32) * W_SCALE, 'W_uk': jax.random.normal(ks[4], (C, KVL), dtype=jnp.float32) * W_SCALE, 'W_uv': jax.random.normal(ks[5], (C, KVL), dtype=jnp.float32) * W_SCALE, 'W_o': jax.random.normal(ks[6], (C, C), dtype=jnp.float32) * W_SCALE}
    _L0_attn_in = _L0_attn_setup()

    def _L0_ffn_setup():
        import jax, jax.numpy as jnp
        import numpy as np
        NUM_GROUPS = 2
        EXPERT_CAPACITY = 80
        NUM_SELECTED = 2
        key = jax.random.key(seed)
        k1, k2, k3, k4 = jax.random.split(key, 4)
        B, S, H, E, F = (4, 256, 128, 8, 512)
        return {'input_emb': jax.random.normal(k1, (B, S, H), dtype=jnp.float32), 'w_router': jax.random.normal(k2, (H, E), dtype=jnp.float32) * 0.02, 'wi': jax.random.normal(k3, (E, H, F), dtype=jnp.float32) * 0.02, 'wo': jax.random.normal(k4, (E, F, H), dtype=jnp.float32) * 0.02}
    _L0_ffn_in = _L0_ffn_setup()
    _d = {'L0_attn_x': _L0_attn_in['x'], 'L0_attn_W_dq': _L0_attn_in['W_dq'], 'L0_attn_W_uq': _L0_attn_in['W_uq'], 'L0_attn_W_dkv': _L0_attn_in['W_dkv'], 'L0_attn_W_uk': _L0_attn_in['W_uk'], 'L0_attn_W_uv': _L0_attn_in['W_uv'], 'L0_attn_W_o': _L0_attn_in['W_o'], 'L0_ffn_w_router': _L0_ffn_in['w_router'], 'L0_ffn_wi': _L0_ffn_in['wi'], 'L0_ffn_wo': _L0_ffn_in['wo']}
    _x0 = _d['L0_attn_x']
    _d['L0_attn_x'] = jax.random.normal(jax.random.fold_in(jax.random.key(seed), 1), (1, 2048, 128), dtype=_x0.dtype)
    del _x0
    return _d

def reference(L0_attn_x, L0_attn_W_dq, L0_attn_W_uq, L0_attn_W_dkv, L0_attn_W_uk, L0_attn_W_uv, L0_attn_W_o, L0_ffn_w_router, L0_ffn_wi, L0_ffn_wo):

    def _L0_attn_ref(x, W_dq, W_uq, W_dkv, W_uk, W_uv, W_o):
        import jax, jax.numpy as jnp
        import numpy as np
        from math import sqrt
        N_HEAD = 16
        W_SCALE = 0.02

        def _reference_tuple_inner(x, W_dq, W_uq, W_dkv, W_uk, W_uv, W_o):
            B, T, C = x.shape
            nh = N_HEAD
            hs = C // nh
            n_kvl = W_dkv.shape[0]
            k_eff = (W_dq.T @ W_uq.T @ W_uk).reshape(nh, hs, n_kvl)
            v_eff = jnp.transpose((W_uv.T @ W_o.T).reshape(n_kvl, nh, hs), (1, 0, 2))
            c_kv = x @ W_dkv.T
            q = x @ W_dq.T @ W_uq.T
            q = q.reshape(B, T, nh, hs)
            q_lat = jnp.einsum('bqhd,hdl->bhql', q, k_eff)
            attn = jnp.einsum('bhql,bkl->bhqk', q_lat, c_kv) / sqrt(hs)
            causal = jnp.tril(jnp.ones((T, T), dtype=bool))
            attn = jnp.where(causal[None, None], attn, -jnp.inf)
            attn = jax.nn.softmax(attn, axis=-1)
            y_lat = jnp.einsum('bhqk,bkl->bhql', attn, c_kv)
            y = jnp.einsum('bhql,hld->bqhd', y_lat, v_eff).reshape(B, T, C)
            return (y, c_kv)
        return _reference_tuple_inner(x, W_dq, W_uq, W_dkv, W_uk, W_uv, W_o)[0]

    def _L0_ffn_ref(input_emb, w_router, wi, wo):
        import jax, jax.numpy as jnp
        import numpy as np
        NUM_GROUPS = 2
        EXPERT_CAPACITY = 80
        NUM_SELECTED = 2
        B, S, H = input_emb.shape
        E = w_router.shape[1]
        G = NUM_GROUPS
        T = B * S // G
        C = EXPERT_CAPACITY
        K = NUM_SELECTED
        x = input_emb.reshape(G, T, H)
        router_logits = jnp.einsum('gth,he->gte', x.astype(jnp.float32), w_router.astype(jnp.float32))
        router_probs = jax.nn.softmax(router_logits, axis=-1)
        gate, idx = jax.lax.top_k(router_probs, K)
        mask = jax.nn.one_hot(idx, E, dtype=jnp.float32)
        mask_kt = jnp.swapaxes(mask, 1, 2).reshape(G, K * T, E)
        pos = jnp.cumsum(mask_kt, axis=1) * mask_kt - 1.0
        pos = jnp.swapaxes(pos.reshape(G, K, T, E), 1, 2)
        disp_k = jax.nn.one_hot(pos, C, dtype=jnp.float32) * mask[..., None]
        dispatch = disp_k.sum(axis=2)
        combine = jnp.einsum('gtk,gtkec->gtec', gate, disp_k)
        expert_in = jnp.einsum('gtec,gth->egch', dispatch, x)
        h = jax.nn.relu(jnp.einsum('egch,ehf->egcf', expert_in, wi))
        expert_out = jnp.einsum('egcf,efh->egch', h, wo)
        y = jnp.einsum('gtec,egch->gth', combine, expert_out)
        return y.reshape(B, S, H)
    x = L0_attn_x
    x = _layernorm(x + _L0_attn_ref(x, L0_attn_W_dq, L0_attn_W_uq, L0_attn_W_dkv, L0_attn_W_uk, L0_attn_W_uv, L0_attn_W_o), axis=-1)
    x = _layernorm(x + _L0_ffn_ref(x, L0_ffn_w_router, L0_ffn_wi, L0_ffn_wo), axis=-1)
    return x

_drawn_inputs = setup_inputs


def setup_inputs(seed=0):
    import zlib

    import numpy as np

    out = dict(_drawn_inputs(seed))
    spreads = {}
    factors = {'L0_attn_W_dq': 8.0,
     'L0_attn_W_uq': 8.0,
     'L0_attn_W_dkv': 8.0,
     'L0_attn_W_uk': 8.0,
     'L0_attn_W_uv': 8.0,
     'L0_attn_W_o': 8.0,
     'L0_ffn_w_router': 6.068,
     'L0_ffn_wi': 6.957,
     'L0_ffn_wo': 5.789}
    for name, (base, spread) in spreads.items():
        noise = np.random.default_rng([zlib.crc32(name.encode()), seed]).standard_normal(out[name].shape)
        drawn = base * np.exp(spread * noise) if base else spread * noise
        out[name] = jnp.asarray(drawn.astype(out[name].dtype))
    for name, factor in factors.items():
        out[name] = (out[name] * factor).astype(out[name].dtype)
    return out
```

```python
from contextlib import ExitStack

import numpy as np

import concourse.bass as bass
from concourse import mybir

P = 128
T, C = 2048, 128
HEADS, HD = 16, 8
LAT = 64
QUERIES = 512
SUPERS = T // QUERIES
TILES = T // P
QT = QUERIES // P
HG = 4
GROUPS = HEADS // HG
UNITS = SUPERS * GROUPS
PARTS = 3
TERMS = PARTS * PARTS
MROW = 126
VC = HD + 1
PRING = 6
LAG = 2
BIG = -1e38

EXPERTS, FF, CAP = 8, 512, 80
MOE_GROUPS = 2
MT = TILES // MOE_GROUPS
SLOTS = EXPERTS * CAP
ZERO_ROW = SLOTS
TRASH = SLOTS + 1
IN_ROWS = TRASH + 2 * MT * P
FC = FF // P
ST = SLOTS // P
EPS = 1e-5

F32, BF16, U32 = mybir.dt.float32, mybir.dt.bfloat16, mybir.dt.uint32
ALU = mybir.AluOpType
ACT = mybir.ActivationFunctionType
AX = mybir.AxisListType


def super_of(u):
    return u // GROUPS


def unit_steps(u):
    return QT * (super_of(u) + 1)


STEPS = [(u, j) for u in range(UNITS) for j in range(unit_steps(u))]
FIRST = [sum(unit_steps(v) for v in range(u)) for u in range(UNITS + 1)]
NSTEP = len(STEPS)


def first_query(u, j):
    return P * max(0, j - QT * super_of(u))


def is_diagonal(u, j):
    return j >= QT * super_of(u)


def max_items(u):
    return [(qt, h, c) for qt in range(QT) for h in range(HG) for c in range(super_of(u) + 1)]


ITEMS_BEFORE = [0]
for _u in range(UNITS):
    ITEMS_BEFORE.append(ITEMS_BEFORE[-1] + len(max_items(_u)))


def woven():
    out = [[] for _ in STEPS]
    for u in range(UNITS - 1):
        n, k = ITEMS_BEFORE[u + 2] - ITEMS_BEFORE[u + 1], unit_steps(u) - 1
        for i in range(n):
            out[FIRST[u] + i * k // n].append(ITEMS_BEFORE[u + 1] + i)
    return out


WOVEN = woven()
ALL_ITEMS = [(u, *it) for u in range(UNITS) for it in max_items(u)]


def schedule():
    out = []
    for u in range(UNITS - 1):
        out.append((FIRST[u + 1] - 2, "max_rows", u + 1))
        out.append((FIRST[u + 1] - 1, "max_turn", u + 1))
    for u in range(UNITS):
        out.append((FIRST[u + 1] - 1 + LAG, "keep_y", u))
    for s in range(SUPERS):
        b = FIRST[GROUPS * (s + 1)] + 3
        for q in range(QT):
            out.append((b + q, "y_turn", QT * s + q))
        out += [(b + 4, "norm_ln", ("attn", s)), (b + 5, "norm_out", ("attn", s)), (b + 6, "x1_turn", s), (b + 7, "logits", s)]
    for g in range(MOE_GROUPS):
        b = FIRST[2 * GROUPS * (g + 1)] + 3 + 8
        out += [(b, "top2", g), (b + 1, "count", g), (b + 1, "slots", g)]
        b += 9 if g == 0 else 2
        out += [(b, "in_turn", (g, 0)), (b, "in_turn", (g, 1))]
        for e in range(EXPERTS):
            out += [(b + 1 + 2 * e, "expert_h", (g, e)), (b + 2 + 2 * e, "expert_o", (g, e))]
        b += 2 * EXPERTS + 1
        out.append((b, "send_back", g))
        b += 8 if g == 0 else 1
        for half in range(2):
            out += [(b, "combine", (g, half)), (b + 1, "norm_ln", ("moe", 2 * g + half)), (b + 2, "norm_out", ("moe", 2 * g + half))]
            b += 3
    return sorted(out, key=lambda x: x[0])


SCHEDULE = schedule()
LAST = max(x[0] for x in SCHEDULE)
TASKS = [[x[1:] for x in SCHEDULE if x[0] == b] for b in range(LAST + 1)]
ORDERED = [x for b in TASKS for x in b]

CONSUMER = {"max_turn": "vector", "y_turn": "vector", "x1_turn": "scalar", "logits": "vector", "count": "vector",
            "in_turn": "scalar", "expert_h": "scalar", "expert_o": "vector"}
TURNS = [x for x in ORDERED if x[0] in CONSUMER]
TURN = {x: n for n, x in enumerate(TURNS)}
TAIL_TURN = sum(1 for b in TASKS[:NSTEP + LAG] for x in b if x[0] in CONSUMER)
TAIL_BANKS = (7, 0, 1, 2, 3, 4, 5)


def bank_of(n):
    return 7 if n < TAIL_TURN else TAIL_BANKS[(n - TAIL_TURN) % len(TAIL_BANKS)]


def emptied(n):
    return sum(1 for m in range(n + 1) if CONSUMER[TURNS[m][0]] == CONSUMER[TURNS[n][0]])


def norm_count(key):
    return [x[1] for x in ORDERED if x[0] == "norm_ln"].index(key) + 1


def program(nc, x_d, wdq_d, wuq_d, wdkv_d, wuk_d, wuv_d, wo_d, router_d, wi_d, wo2_d, out_d):
    ctx = ExitStack()
    with ctx:
        def sb(name, shape, dt=F32):
            return ctx.enter_context(nc.sbuf_tensor(name, shape, dt))

        def sem(name):
            return ctx.enter_context(nc.semaphore(name))

        parts_d = [nc.dram_tensor(f"parts_{n}", (PARTS, C, T), BF16, kind="Internal").ap() for n in "kq"]
        exp_in_d = [nc.dram_tensor(f"exp_in_{g}", (IN_ROWS, C), F32, kind="Internal").ap() for g in range(MOE_GROUPS)]
        exp_out_d = [nc.dram_tensor(f"exp_out_{g}", (SLOTS + 1, C), F32, kind="Internal").ap() for g in range(MOE_GROUPS)]

        kT = sb("kT", [P, HEADS, T], BF16)
        qT = [sb(f"qT{i}", [P, HEADS, QUERIES], BF16) for i in range(2)]
        v = sb("v", [P, TILES, HEADS, VC])
        probs = [sb(f"probs{i}", [P, 2, QUERIES]) for i in range(PRING)]
        x = sb("x", [P, TILES, C])
        x1 = sb("x1", [P, TILES, C])
        yT = [sb(f"yT{g}", [P, QUERIES]) for g in range(GROUPS)]
        wi = sb("wi", [P, EXPERTS, FF])
        wo2 = sb("wo2", [P, EXPERTS, FC, C])
        xT = wo2[:, :, :, :].rearrange("p e f c -> p (e f c)")[:, 0:T]
        wi_flat = wi[:, :, :].rearrange("p e f -> p (e f)")
        rest = [wi_flat[:, i * QUERIES:(i + 1) * QUERIES] for i in range(2)]
        split = [wi_flat[:, 1024 + i * 768:1024 + (i + 1) * 768].bitcast(BF16).rearrange("p (a t) -> p a t", a=PARTS)
                 for i in range(2)]

        router = sb("router", [C, EXPERTS])
        small = wo2[:, :, :, :].rearrange("p e f c -> p (e f c)")[:, T:2 * T]

        def early(i, rows, cols):
            return small[0:rows, i * C:i * C + cols]

        wdq, wuq, wdkv, wuk = early(0, LAT, C), early(1, C, LAT), early(2, LAT, C), early(3, C, LAT)
        wuv, wo, wuqT, woT = early(4, C, LAT), early(5, C, C), early(6, LAT, C), early(7, C, C)
        uq_uk, keffT, veff = early(8, LAT, LAT), early(9, LAT, C), early(10, LAT, C)
        qw, kw, vw = early(11, C, C), early(12, C, C), early(13, C, C)

        ident = sb("ident", [P, P])
        ident16 = sb("ident16", [P, P], BF16)
        ones16 = sb("ones16", [P, P], BF16)
        tri16 = sb("tri16", [P, P], BF16)
        later16 = sb("later16", [P, P], BF16)
        causal = sb("causal", [P, QUERIES])
        iota_e = sb("iota_e", [P, EXPERTS])
        trash1 = sb("trash1", [P, 2 * MT])

        unused = [sb(f"unused{i}", [P, QUERIES], BF16) for i in range(2)]
        part_max = [sb(f"part_max{i}", [P, QT * HG, SUPERS]) for i in range(2)]
        neg_max = sb("neg_max", [P, QT * HG])
        max16 = [sb(f"max16_{i}", [P, QT, 2, HG], BF16) for i in range(2)]
        maxT = [sb(f"maxT{i}", [2 * HG, QUERIES], BF16) for i in range(2)]

        recip = sb("recip", [P, HEADS, 1])
        res = sb("res", [P, QT, C])
        stats = sb("stats", [P, QT, 6])
        mv = sb("mv", [P, QT, 2])
        var = sb("var", [P, QT])
        lnv = sb("lnv", [P, QT])
        rs0 = sb("rs0", [P, QT])
        rs = sb("rs", [P, QT])
        nt = sb("nt", [P, QT])
        lg = sb("lg", [P, MT, EXPERTS])
        top = sb("top", [P, MT, 8])
        top_i = sb("top_i", [P, MT, 8], U32)
        expert = sb("expert", [P, 2, MT])
        mask16 = sb("mask16", [P, 2 * MT, EXPERTS], BF16)
        lgm = sb("lgm", [P, MT, 8])
        ex = sb("ex", [P, MT, 8])
        exs = sb("exs", [P, MT])
        exr = sb("exr", [P, MT])
        gate = sb("gate", [P, 2, MT])
        cw = sb("cw", [P, 2 * MT, EXPERTS])
        place = sb("place", [P, 2 * MT])
        slot = sb("slot", [P, 2 * MT])
        over = sb("over", [P, 2 * MT])
        away = sb("away", [P, 2 * MT])
        slot_in = sb("slot_in", [P, 2 * MT], U32)
        slot_out = sb("slot_out", [P, 2 * MT], U32)
        einT = sb("einT", [P, SLOTS])
        x1T = einT[:, 0:QUERIES]
        hT = [sb(f"hT{i}", [P, FC, CAP]) for i in range(2)]
        back2 = sb("back2", [P, MT, C])
        ein = back2[:, 0:ST, :]

        scT = [ctx.enter_context(nc.psum_tensor(f"scT{i}", [P, 2, QUERIES], F32)) for i in range(2)]
        sc = [ctx.enter_context(nc.psum_tensor(f"sc{i}", [P, QUERIES], F32)) for i in range(2)]
        acc = ctx.enter_context(nc.psum_tensor("acc", [P, QUERIES], F32))
        ms = ctx.enter_context(nc.psum_tensor("ms", [P, QUERIES], F32))
        BANKS = [scT[0][:, 0, :], scT[0][:, 1, :], scT[1][:, 0, :], scT[1][:, 1, :], sc[0][:, :], sc[1][:, :], acc[:, :], ms[:, :]]

        s_w = sem("s_w")
        s_router = sem("s_router")
        s_x = [sem(f"s_x{i}") for i in range(SUPERS)]
        s_ffw = sem("s_ffw")
        s_const = sem("s_const")
        s_const_v = sem("s_const_v")
        s_rows = sem("s_rows")
        w_made = sem("w_made")
        w_kept = sem("w_kept")
        xT_made = sem("xT_made")
        xT_kept = sem("xT_kept")
        kq_made = sem("kq_made")
        kq_hi = sem("kq_hi")
        kq_r1 = sem("kq_r1")
        kq_mid = sem("kq_mid")
        kq_lo = sem("kq_lo")
        parts_out = [sem(f"parts_out{i}") for i in range(2)]
        v_made = sem("v_made")
        v_kept = sem("v_kept")
        kq_in = [sem(f"kq_in{i}") for i in range(SUPERS)]
        sc_made = sem("sc_made")
        sc_used = sem("sc_used")
        max_done = sem("max_done")
        maxT_kept = sem("maxT_kept")
        max_in = [sem(f"max_in{i}") for i in range(2)]
        scT_made = sem("scT_made")
        exp_done = sem("exp_done")
        pv_done = sem("pv_done")
        y_kept = sem("y_kept")
        turn_made = sem("turn_made")
        empty = {"vector": sem("empty_v"), "scalar": sem("empty_s")}
        var_ready = sem("var_ready")
        rs_ready = sem("rs_ready")
        x1_done = sem("x1_done")
        lgm_done = sem("lgm_done")
        ex_done = sem("ex_done")
        mask_done = sem("mask_done")
        slots_done = sem("slots_done")
        cleared = sem("cleared")
        scattered = [sem(f"scattered{g}") for g in range(MOE_GROUPS)]
        ein_in = sem("ein_in")
        o_kept = sem("o_kept")
        o_out = sem("o_out")
        gathered = [sem(f"gathered{g}") for g in range(MOE_GROUPS)]
        out_ready = sem("out_ready")
        s_out = sem("s_out")
        chain = sem("chain")

        def turn_bank(task):
            return BANKS[bank_of(TURN[task])]

        def take_bank(eng, task):
            n = TURN[task]
            before = [m for m in range(n) if bank_of(m) == bank_of(n)]
            if before:
                eng.wait_ge(empty[CONSUMER[TURNS[before[-1]][0]]], emptied(before[-1]))

        def token_rows(d, a, b):
            return d[a * P:b * P, :].rearrange("(n p) c -> p n c", p=P)

        block = ctx.enter_context(nc.Block())

        @block.sync
        def _(sp):
            sp.dma_start(x[:, 0:QT, :], token_rows(x_d, 0, QT)).then_inc(s_x[0], 16)
            for dst, src in ((wuq, wuq_d), (wuk, wuk_d), (wo, wo_d), (wdq, wdq_d), (wuv, wuv_d), (wdkv, wdkv_d)):
                sp.dma_start(dst, src).then_inc(s_w, 16)
            for i in range(1, SUPERS):
                sp.dma_start(x[:, i * QT:(i + 1) * QT, :], token_rows(x_d, i * QT, (i + 1) * QT)).then_inc(s_x[i], 16)
            sp.dma_start(router[:, :], router_d).then_inc(s_router, 16)
            sp.wait_ge(s_const, 3)
            for g in range(MOE_GROUPS):
                sp.dma_start(exp_in_d[g][0:SLOTS, :].rearrange("(n p) c -> p n c", p=P),
                             causal[:, 0:C].unsqueeze(1).to_broadcast([P, ST, C])).then_inc(cleared, 16)
                sp.dma_start(exp_out_d[g][ZERO_ROW:ZERO_ROW + 1, :], causal[0:1, 0:C]).then_inc(cleared, 16)

            def load_products(i, n):
                dst = kT[:, :, i * QUERIES:(i + 1) * QUERIES] if n == 0 else qT[i % 2][:, :, :]
                for j in range(TERMS):
                    part = j // PARTS if n == 0 else j % PARTS
                    src = parts_d[n][part].rearrange("(h d) t -> d h t", d=HD)[:, :, i * QUERIES:(i + 1) * QUERIES]
                    sp.dma_start(dst[j * HD:(j + 1) * HD, :, :], src).then_inc(kq_in[i], 16)

            for i in range(SUPERS):
                for n in range(2):
                    sp.wait_ge(kq_lo, 2 * i + n + 1)
                    sp.wait_ge(kq_mid, 2 * i + n + 1)
                    sp.dma_start(parts_d[n].rearrange("a c t -> c a t")[:, :, i * QUERIES:(i + 1) * QUERIES],
                                 split[n][:, :, :]).then_inc(parts_out[n], 16)
                for n in range(2):
                    if n == 1 and i >= 2:
                        continue
                    sp.wait_ge(s_rows, (1, 4, 5, 6)[i] if n == 0 else (2, 3)[i])
                    sp.wait_ge(parts_out[n], 16 * (i + 1))
                    load_products(i, n)
            sp.wait_ge(parts_out[1], 16 * SUPERS)
            sp.wait_ge(parts_out[0], 16 * SUPERS)
            sp.wait_ge(v_made, SUPERS)
            sp.dma_start(wi[:, :, :], wi_d.rearrange("e h f -> h e f")).then_inc(s_ffw, 16)
            sp.dma_start(wo2[:, :, :, :], wo2_d.rearrange("e (f p) h -> p e f h", p=P)).then_inc(s_ffw, 16)

            def max_to_rows(u):
                sp.wait_ge(maxT_kept, u + 1)
                q, g = qT[super_of(u) % 2], u % GROUPS
                for part in range(2):
                    sp.dma_start(q[MROW + part:MROW + part + 1, g * HG:(g + 1) * HG, :],
                                 maxT[u % 2][part * HG:(part + 1) * HG, :]).then_inc(max_in[u % 2], 16)

            max_to_rows(0)
            for b in range(LAST + 1):
                for name, arg in TASKS[b]:
                    if name == "max_turn":
                        max_to_rows(arg)
                        if arg in (GROUPS, 2 * GROUPS):
                            s = super_of(arg) + 1
                            sp.wait_ge(scT_made, 2 * FIRST[arg])
                            load_products(s, 1)
                    if name == "expert_o" and arg[1] in (EXPERTS // 2 - 1, EXPERTS - 1):
                        g, e = arg
                        e0 = e + 1 - EXPERTS // 2
                        sp.wait_ge(o_kept, EXPERTS * g + e + 1)
                        sp.dma_start(exp_out_d[g][e0 * CAP:(e + 1) * CAP, :].rearrange("(e p) h -> p e h", p=CAP),
                                     x[0:CAP, g * MT + e0:g * MT + e + 1, :]).then_inc(o_out, 16)
                    if name == "slots":
                        sp.wait_ge(scattered[arg], 16 * 2 * MT)
                        if arg:
                            sp.wait_ge(out_ready, 2 * arg)
                        sp.dma_start(ein, exp_in_d[arg][0:SLOTS, :].rearrange("(n p) c -> p n c", p=P)).then_inc(ein_in, 16)
                    if name == "norm_out" and arg[0] == "moe":
                        k = arg[1]
                        sp.wait_ge(out_ready, k + 1)
                        sp.dma_start(token_rows(out_d, k * QT, (k + 1) * QT),
                                     x[:, k * QT:(k + 1) * QT, :]).then_inc(s_out, 16)
            sp.wait_ge(s_out, 16 * SUPERS)

        @block.gpsimd
        def _(pool):
            nc.gpsimd.memset(ident[:, :], 0.0).then_inc(s_const, 1)
            nc.gpsimd.memset(ones16[:, :], 1.0).then_inc(s_const, 1)
            nc.gpsimd.memset(causal[:, :], 0.0).then_inc(s_const, 1)
            pool.wait_ge(s_const, 3)
            nc.gpsimd.affine_select(out=ident[:, :], in_=ident[:, :], compare_op=ALU.not_equal, fill=1.0, base=0,
                                    pattern=[[-1, P]], channel_multiplier=1).then_inc(s_const, 1)
            pool.wait_ge(s_const, 4)
            nc.gpsimd.tensor_copy(ident16[:, :], ident[:, :]).then_inc(s_const, 1)
            nc.gpsimd.affine_select(out=tri16[:, :], in_=ones16[:, :], compare_op=ALU.is_ge, fill=0.0, base=0,
                                    pattern=[[1, P]], channel_multiplier=-1).then_inc(s_const, 1)
            nc.gpsimd.memset(later16[:, :], 0.0).then_inc(s_const, 1)
            pool.wait_ge(s_const, 7)
            nc.gpsimd.affine_select(out=later16[:, :], in_=later16[:, :], compare_op=ALU.is_ge, fill=BIG, base=0,
                                    pattern=[[1, P]], channel_multiplier=-1).then_inc(s_const, 1)
            tri = causal[:, QUERIES - P:QUERIES]
            nc.gpsimd.affine_select(out=tri, in_=tri, compare_op=ALU.is_ge, fill=BIG, base=0,
                                    pattern=[[-1, P]], channel_multiplier=1).then_inc(s_const, 1)
            one_pair = 0x3F803F80

            def fill_k(i):
                rows = kT[P // 2:P, :, i * QUERIES:(i + 1) * QUERIES].bitcast(U32)
                nc.gpsimd.memset(rows, one_pair).then_inc(s_rows, 1)

            pool.wait_ge(s_const, 9)
            fill_k(0)
            for q in qT:
                nc.gpsimd.memset(q[P // 2:P, :, :].bitcast(U32), 0).then_inc(s_rows, 1)
            for i in range(1, SUPERS):
                fill_k(i)
            pool.wait_ge(s_rows, 6)
            nc.gpsimd.iota(iota_e[:, :], [[1, EXPERTS]], base=0, channel_multiplier=0,
                           allow_small_or_imprecise_dtypes=True).then_inc(s_const, 1)
            nc.gpsimd.iota(trash1[:, :], [[P, 2 * MT]], base=TRASH + 1, channel_multiplier=1,
                           allow_small_or_imprecise_dtypes=True).then_inc(s_const, 1)

            def scatter(g):
                pool.wait_ge(slots_done, g + 1)
                pool.wait_ge(cleared, 16 * 4)
                for n in range(2 * MT):
                    pool.indirect_dma_start(exp_in_d[g][:, :], bass.IndirectOffsetOnAxis(slot_in[:, n:n + 1], 0),
                                            x1[:, g * MT + n % MT, :], None).then_inc(scattered[g], 16)

            def gather(g):
                pool.wait_ge(o_out, 16 * 2 * (g + 1))
                for n in range(2 * MT):
                    dst = x[:, g * MT + n, :] if n < MT else back2[:, n - MT, :]
                    pool.indirect_dma_start(dst, None, exp_out_d[g][:, :],
                                            bass.IndirectOffsetOnAxis(slot_out[:, n:n + 1], 0)).then_inc(gathered[g], 16)

            for b in range(LAST + 1):
                for name, arg in TASKS[b]:
                    if name == "slots":
                        scatter(arg)
                    if name == "send_back":
                        gather(arg)

        @block.scalar
        def _(act):
            nc.scalar.preload_act_table_set("natural_log_exp_and_others")
            for i in range(SUPERS):
                for n in range(2):
                    k = 2 * i + n
                    act.wait_ge(kq_made, k + 1)
                    if i >= 1:
                        act.wait_ge(parts_out[n], 16 * i)
                    nc.scalar.activation(split[n][:, 0, :], sc[n][:, :], ACT.Copy).then_inc(kq_hi, 1)
                    act.wait_ge(kq_r1, k + 1)
                    nc.scalar.activation(split[n][:, 1, :], rest[n], ACT.Copy).then_inc(kq_mid, 1)
                act.wait_ge(v_made, i + 1)
                act.wait_ge(s_const_v, 1)
                nc.scalar.activation(v[:, i * QT:(i + 1) * QT, :, 0:HD],
                                     scT[1][:, i % 2, :].rearrange("p (n h d) -> p n h d", n=QT, h=HEADS), ACT.Copy).then_inc(v_kept, 1)

            def exps(b):
                u, j = STEPS[b]
                width = QUERIES - first_query(u, j)
                for half in range(2):
                    n = 2 * b + half
                    act.wait_ge(scT_made, n + 1)
                    if n >= PRING:
                        act.wait_ge(pv_done, (n - PRING) // 2 + 1)
                    nc.scalar.activation(probs[n % PRING][:, :, 0:width], scT[n % 2][:, :, 0:width], ACT.Exp).then_inc(exp_done, 1)

            for b in range(LAST + 1):
                if b < NSTEP:
                    exps(b)
                for name, arg in TASKS[b]:
                    if name == "keep_y":
                        act.wait_ge(pv_done, FIRST[arg + 1])
                        if arg >= GROUPS:
                            act.wait_ge(turn_made, TURN[("y_turn", QT * super_of(arg) - 1)] + 1)
                        nc.scalar.activation(yT[arg % GROUPS][:, :], acc[:, :], ACT.Copy).then_inc(y_kept, 1)
                    if name == "norm_ln":
                        k = norm_count(arg)
                        act.wait_ge(var_ready, k)
                        nc.scalar.activation(lnv[:, :], var[:, :], ACT.Ln).then_inc(rs_ready, 1)
                        act.wait_ge(rs_ready, 2 * k - 1)
                        nc.scalar.activation(rs0[:, :], lnv[:, :], ACT.Exp, scale=-0.5).then_inc(rs_ready, 1)
                    if name == "x1_turn":
                        act.wait_ge(turn_made, TURN[(name, arg)] + 1)
                        if arg:
                            last = ("expert_h", (arg // 2 - 1, EXPERTS - 1)) if arg % 2 == 0 else ("logits", arg - 1)
                            act.wait_ge(turn_made, TURN[last] + 1)
                        nc.scalar.activation(x1T, turn_bank((name, arg)), ACT.Copy).then_inc(empty["scalar"], 1)
                    if name == "top2":
                        act.wait_ge(lgm_done, arg + 1)
                        nc.scalar.activation(ex[:, :, :], lgm[:, :, :], ACT.Exp).then_inc(ex_done, 1)
                    if name == "in_turn":
                        act.wait_ge(turn_made, TURN[(name, arg)] + 1)
                        act.wait_ge(turn_made, TURN[("logits", 2 * arg[0] + 1)] + 1)
                        n = (QT, 1)[arg[1]] * P
                        nc.scalar.activation(einT[:, arg[1] * QUERIES:arg[1] * QUERIES + n], turn_bank((name, arg))[:, 0:n],
                                             ACT.Copy).then_inc(empty["scalar"], 1)
                    if name == "expert_h":
                        act.wait_ge(turn_made, TURN[(name, arg)] + 1)
                        if arg[0] * EXPERTS + arg[1] >= 2:
                            e = arg[0] * EXPERTS + arg[1] - 2
                            act.wait_ge(turn_made, TURN[("expert_o", (e // EXPERTS, e % EXPERTS))] + 1)
                        nc.scalar.activation(hT[arg[1] % 2][:, :, :], turn_bank((name, arg))[:, 0:FC * CAP].rearrange("p (f t) -> p f t", f=FC),
                                             ACT.Relu).then_inc(empty["scalar"], 1)

        @block.vector
        def _(dve):
            made = [0]

            def link(ins):
                made[0] += 1
                ins.then_inc(chain, 1)
                dve.wait_ge(chain, made[0])

            nc.vector.memset(v[:, :, :, HD:VC], 1.0).then_inc(s_const_v, 1)
            dve.wait_ge(w_made, 1)
            nc.vector.tensor_copy(wuqT, sc[0][0:LAT, 0:C]).then_inc(w_kept, 1)
            nc.vector.tensor_copy(woT, sc[0][:, C:2 * C]).then_inc(w_kept, 1)
            nc.vector.tensor_copy(uq_uk, sc[1][0:LAT, 0:LAT]).then_inc(w_kept, 1)
            dve.wait_ge(w_made, 2)
            nc.vector.tensor_scalar(qw, acc[:, 0:C], float(HD) ** -0.5, None, ALU.mult).then_inc(w_kept, 1)
            nc.vector.tensor_copy(keffT, ms[0:LAT, 0:C]).then_inc(w_kept, 1)
            nc.vector.tensor_copy(veff, ms[0:LAT, C:2 * C]).then_inc(w_kept, 1)
            dve.wait_ge(w_made, 3)
            nc.vector.tensor_copy(kw, scT[1][:, 1, 0:C]).then_inc(w_kept, 1)
            nc.vector.tensor_copy(vw, scT[1][:, 1, C:2 * C]).then_inc(w_kept, 1)
            nc.vector.memset(acc[:, :], 0.0).then_inc(s_const_v, 1)
            for i in range(SUPERS):
                dve.wait_ge(xT_made, i + 1)
                nc.vector.tensor_copy(xT[:, i * QUERIES:(i + 1) * QUERIES], scT[0][:, i % 2, :]).then_inc(xT_kept, 1)
                if i == 0:
                    continue
                for n in range(2):
                    k = 2 * (i - 1) + n
                    dve.wait_ge(kq_hi, k + 1)
                    if k >= 2:
                        dve.wait_ge(kq_mid, k - 1)
                    nc.vector.tensor_tensor(rest[n], sc[n][:, :], split[n][:, 0, :], ALU.subtract).then_inc(kq_r1, 1)
                for n in range(2):
                    k = 2 * (i - 1) + n
                    dve.wait_ge(kq_r1, k + 1)
                    dve.wait_ge(kq_mid, k + 1)
                    nc.vector.tensor_tensor(split[n][:, 2, :], rest[n], split[n][:, 1, :], ALU.subtract).then_inc(kq_lo, 1)
            for n in range(2):
                k = 2 * (SUPERS - 1) + n
                dve.wait_ge(kq_hi, k + 1)
                dve.wait_ge(kq_mid, k - 1)
                nc.vector.tensor_tensor(rest[n], sc[n][:, :], split[n][:, 0, :], ALU.subtract).then_inc(kq_r1, 1)
            for n in range(2):
                k = 2 * (SUPERS - 1) + n
                dve.wait_ge(kq_r1, k + 1)
                dve.wait_ge(kq_mid, k + 1)
                nc.vector.tensor_tensor(split[n][:, 2, :], rest[n], split[n][:, 1, :], ALU.subtract).then_inc(kq_lo, 1)

            def row_max(i):
                u, qt, h, c = ALL_ITEMS[i]
                dve.wait_ge(sc_made, i + 1)
                dst = part_max[u % 2][:, qt * HG + h, c:c + 1]
                if c < super_of(u):
                    nc.vector.tensor_reduce(dst, sc[i % 2][:, :], AX.X, ALU.max).then_inc(sc_used, 1)
                else:
                    w = (qt + 1) * P
                    if i >= 2:
                        dve.wait_ge(sc_used, i - 1)
                    nc.vector.tensor_tensor_reduce(unused[i % 2][:, 0:w], sc[i % 2][:, 0:w], causal[:, QUERIES - w:QUERIES], 1.0, 3 * BIG,
                                                   ALU.add, ALU.max, dst).then_inc(sc_used, 1)

            def max_rows(u):
                dve.wait_ge(sc_used, ITEMS_BEFORE[u + 1])
                if u >= 2:
                    dve.wait_ge(turn_made, 0 if u < 3 else TURN[("max_turn", u - 2)] + 1) if u >= 3 else None
                link(nc.vector.tensor_reduce(neg_max[:, :], part_max[u % 2][:, :, 0:super_of(u) + 1], AX.X, ALU.max, negate=True))
                m = max16[u % 2]
                nm = neg_max[:, :].rearrange("p (q h) -> p q h", q=QT)
                link(nc.vector.tensor_copy(m[:, :, 0, :], nm))
                nc.vector.tensor_tensor(m[:, :, 1, :], nm, m[:, :, 0, :], ALU.subtract).then_inc(max_done, 1)

            def keep_maxT(u, bank):
                if u >= 2:
                    dve.wait_ge(max_in[u % 2], 32 * (u // 2))
                return nc.vector.tensor_copy(maxT[u % 2][:, :], bank.bitcast(BF16)[0:2 * HG, 0:QUERIES])

            dve.wait_ge(s_const, 11)
            for i in range(ITEMS_BEFORE[1]):
                row_max(i)
            max_rows(0)
            dve.wait_ge(w_made, 4)
            keep_maxT(0, ms[:, :]).then_inc(maxT_kept, 1)

            def y_turn(tile):
                s, q = divmod(tile, QT)
                bank = turn_bank(("y_turn", tile)).rearrange("p (h e) -> p h e", h=HEADS)
                dve.wait_ge(turn_made, TURN[("y_turn", tile)] + 1)
                link(nc.vector.reciprocal(recip[:, :, :], bank[:, :, HD:VC]))
                r = res[:, q, :]
                made[0] += 1
                nc.vector.tensor_tensor(r.rearrange("p (h d) -> p h d", h=HEADS), bank[:, :, 0:HD],
                                        recip[:, :, :].to_broadcast([P, HEADS, HD]), ALU.mult).then_inc(chain, 1)
                dve.wait_ge(chain, made[0])
                nc.vector.sem_inc(empty["vector"], 1)
                link(nc.vector.tensor_tensor(r, r, x[:, tile, :], ALU.add))
                link(nc.vector.bn_stats(stats[:, q, :], r))
                link(nc.vector.bn_aggr(mv[:, q, :], stats[:, q, :]))

            def norm_out(kind, k):
                n = norm_count((kind, k))
                dve.wait_ge(rs_ready, 2 * n)
                link(nc.vector.tensor_tensor(nt[:, :], rs0[:, :], rs0[:, :], ALU.mult))
                link(nc.vector.tensor_tensor(nt[:, :], nt[:, :], var[:, :], ALU.mult))
                link(nc.vector.tensor_scalar(nt[:, :], nt[:, :], -0.5, 1.5, ALU.mult, ALU.add))
                link(nc.vector.tensor_tensor(rs[:, :], rs0[:, :], nt[:, :], ALU.mult))
                for q in range(QT):
                    if kind == "attn":
                        src, dst = res[:, q, :], x1[:, k * QT + q, :]
                    else:
                        src = dst = x[:, k * QT + q, :]
                    ins = nc.vector.tensor_scalar(dst, src, mv[:, q, 0:1], rs[:, q:q + 1], ALU.subtract, ALU.mult)
                    if q == QT - 1:
                        ins.then_inc(x1_done if kind == "attn" else out_ready, 1)

            def top2(g):
                for i in range(MT):
                    ins = nc.vector.max(top[:, i, :], lg[:, i, :])
                link(ins)
                if g:
                    dve.wait_ge(gathered[g - 1], 16 * 2 * MT)
                for i in range(MT):
                    nc.vector.max_index(top_i[:, i, :], top[:, i, :], lg[:, i, :])
                nc.vector.tensor_tensor(lgm[:, :, :], top[:, :, :], top[:, :, 0:1].to_broadcast([P, MT, 8]),
                                        ALU.subtract).then_inc(lgm_done, 1)
                link(nc.vector.memset(exs[:, :], 0.0))
                link(nc.vector.tensor_copy(expert[:, :, :], top_i[:, :, 0:2].rearrange("p i k -> p k i")))
                nc.vector.tensor_tensor(mask16[:, :, :], iota_e[:, :].unsqueeze(1).to_broadcast([P, 2 * MT, EXPERTS]),
                                        expert[:, :, :].rearrange("p k i -> p (k i)").unsqueeze(2).to_broadcast([P, 2 * MT, EXPERTS]),
                                        ALU.is_equal).then_inc(mask_done, 1)
                dve.wait_ge(ex_done, g + 1)
                link(nc.vector.tensor_reduce(exs[:, :], ex[:, :, :], AX.X, ALU.add))
                link(nc.vector.reciprocal(exr[:, :], exs[:, :]))
                nc.vector.tensor_tensor(gate[:, :, :], ex[:, :, 0:2].rearrange("p i k -> p k i"),
                                        exr[:, :].unsqueeze(1).to_broadcast([P, 2, MT]), ALU.mult).then_inc(chain, 1)
                made[0] += 1

            def slots(g):
                dve.wait_ge(turn_made, TURN[("count", g)] + 1)
                counts = turn_bank(("count", g))[:, 0:2 * MT * EXPERTS].rearrange("p (n e) -> p n e", e=EXPERTS)
                made[0] += 1
                nc.vector.tensor_tensor(cw[:, :, :], counts, mask16[:, :, :], ALU.mult).then_inc(chain, 1)
                dve.wait_ge(chain, made[0])
                nc.vector.sem_inc(empty["vector"], 1)
                link(nc.vector.tensor_reduce(place[:, :], cw[:, :, :], AX.X, ALU.add))
                link(nc.vector.scalar_tensor_tensor(slot[:, :], expert[:, :, :].rearrange("p k i -> p (k i)"), float(CAP), place[:, :],
                                                    ALU.mult, ALU.add))
                link(nc.vector.tensor_scalar(over[:, :], place[:, :], float(CAP), None, ALU.is_gt))
                link(nc.vector.tensor_tensor(away[:, :], trash1[:, :], slot[:, :], ALU.subtract))
                link(nc.vector.tensor_tensor(away[:, :], away[:, :], over[:, :], ALU.mult))
                link(nc.vector.tensor_tensor(slot[:, :], slot[:, :], away[:, :], ALU.add))
                nc.vector.tensor_scalar(slot_out[:, :], slot[:, :], float(ZERO_ROW + 1), -1.0, ALU.min, ALU.add)
                nc.vector.tensor_scalar(slot_in[:, :], slot[:, :], -1.0, None, ALU.add).then_inc(slots_done, 1)

            def combine(g, half):
                dve.wait_ge(gathered[g], 16 * 2 * MT)
                for q in range(QT):
                    i = half * QT + q
                    a, b = x[:, g * MT + i, :], back2[:, i, :]
                    link(nc.vector.scalar_tensor_tensor(a, a, gate[:, 0, i:i + 1], x1[:, g * MT + i, :], ALU.mult, ALU.add))
                    link(nc.vector.scalar_tensor_tensor(a, b, gate[:, 1, i:i + 1], a, ALU.mult, ALU.add))
                    link(nc.vector.bn_stats(stats[:, q, :], a))
                    link(nc.vector.bn_aggr(mv[:, q, :], stats[:, q, :]))

            for b in range(LAST + 1):
                if b < NSTEP:
                    for i in WOVEN[b]:
                        row_max(i)
                for name, arg in TASKS[b]:
                    if name == "max_rows":
                        max_rows(arg)
                    if name == "max_turn":
                        dve.wait_ge(turn_made, TURN[(name, arg)] + 1)
                        made[0] += 1
                        keep_maxT(arg, turn_bank((name, arg))).then_inc(maxT_kept, 1)
                        dve.wait_ge(maxT_kept, arg + 1)
                        nc.vector.sem_inc(empty["vector"], 1)
                        made[0] -= 1
                    if name == "y_turn":
                        y_turn(arg)
                    if name == "norm_ln":
                        nc.vector.tensor_scalar(var[:, :], mv[:, :, 1], EPS, None, ALU.add).then_inc(var_ready, 1)
                    if name == "norm_out":
                        norm_out(*arg)
                    if name == "logits":
                        dve.wait_ge(turn_made, TURN[(name, arg)] + 1)
                        nc.vector.tensor_copy(lg[:, (arg % 2) * QT:(arg % 2 + 1) * QT, :],
                                              turn_bank((name, arg))[:, 0:QT * EXPERTS].rearrange("p (q e) -> p q e", e=EXPERTS)
                                              ).then_inc(empty["vector"], 1)
                    if name == "top2":
                        dve.wait_ge(empty["vector"], emptied(TURN[("logits", 2 * arg + 1)]))
                        top2(arg)
                    if name == "slots":
                        slots(arg)
                    if name == "expert_o":
                        g, e = arg
                        dve.wait_ge(turn_made, TURN[(name, arg)] + 1)
                        nc.vector.tensor_copy(x[0:CAP, g * MT + e, :], turn_bank((name, arg))[0:CAP, 0:C]).then_inc(o_kept, 1)
                        dve.wait_ge(o_kept, EXPERTS * g + e + 1)
                        nc.vector.sem_inc(empty["vector"], 1)
                    if name == "combine":
                        combine(*arg)

        @block.tensor
        def _(pe):
            pe.wait_ge(s_const, 4)
            pe.wait_ge(s_w, 16 * 6)
            nc.tensor.transpose(sc[0][0:LAT, 0:C], wuq, ident[:, :])
            nc.tensor.transpose(sc[0][:, C:2 * C], wo, ident[:, :])
            nc.tensor.matmul(sc[1][0:LAT, 0:LAT], wuq, wuk, start=True, stop=True).then_inc(w_made, 1)

            def turn_x(i):
                pe.wait_ge(s_x[i], 16)
                if i >= 2:
                    pe.wait_ge(xT_kept, i - 1)
                for q in range(QT):
                    ins = nc.tensor.transpose(scT[0][:, i % 2, q * P:(q + 1) * P], x[:, i * QT + q, :], ident[:, :])
                ins.then_inc(xT_made, 1)

            turn_x(0)
            pe.wait_ge(w_kept, 3)
            nc.tensor.matmul(acc[:, 0:C], wdq, wuqT, start=True, stop=True)
            nc.tensor.matmul(ms[0:LAT, 0:C], uq_uk, wdq, start=True, stop=True)
            nc.tensor.matmul(ms[0:LAT, C:2 * C], wuv, woT, start=True, stop=True).then_inc(w_made, 1)
            turn_x(1)
            pe.wait_ge(w_kept, 6)
            nc.tensor.matmul(scT[1][:, 1, 0:C], wdkv, keffT, start=True, stop=True)
            nc.tensor.matmul(scT[1][:, 1, C:2 * C], wdkv, veff, start=True, stop=True).then_inc(w_made, 1)
            pe.wait_ge(w_kept, 8)
            for i in range(SUPERS):
                pe.wait_ge(xT_kept, i + 1)
                xt = xT[:, i * QUERIES:(i + 1) * QUERIES]
                for n, w in enumerate((kw, qw)):
                    if i >= 1:
                        pe.wait_ge(kq_r1, 2 * (i - 1) + n + 1)
                    nc.tensor.matmul(sc[n][:, :], w, xt, start=True, stop=True).then_inc(kq_made, 1)
                if i >= 2:
                    pe.wait_ge(v_kept, i - 1)
                for q in range(QT):
                    ins = nc.tensor.matmul(scT[1][:, i % 2, q * P:(q + 1) * P], xT[:, (i * QT + q) * P:(i * QT + q + 1) * P], vw,
                                           start=True, stop=True)
                ins.then_inc(v_made, 1)
                if i + 2 < SUPERS:
                    turn_x(i + 2)

            def scores_for_max(i):
                u, qt, h, c = ALL_ITEMS[i]
                s, head = super_of(u), u % GROUPS * HG + h
                if (i == ITEMS_BEFORE[u]) and u % GROUPS == 0:
                    pe.wait_ge(kq_in[s], 16 * 2 * TERMS)
                if i >= 2:
                    pe.wait_ge(sc_used, i - 1)
                w = QUERIES if c < s else (qt + 1) * P
                nc.tensor.matmul(sc[i % 2][:, 0:w], qT[s % 2][0:MROW, head, qt * P:(qt + 1) * P],
                                 kT[0:MROW, head, c * QUERIES:c * QUERIES + w], start=True, stop=True).then_inc(sc_made, 1)

            def turn_max(u, bank):
                pe.wait_ge(max_done, u + 1)
                for q in range(QT):
                    ins = nc.tensor.transpose(bank.bitcast(BF16)[0:2 * HG, q * P:(q + 1) * P],
                                              max16[u % 2][:, q, :, :].rearrange("p a h -> p (a h)"), ident16[:, :])
                return ins

            def scores(b):
                u, j = STEPS[b]
                s, off = super_of(u), first_query(u, j)
                if j == 0:
                    pe.wait_ge(max_in[u % 2], 32 * (u // 2 + 1))
                for half in range(2):
                    n = 2 * b + half
                    if n >= 2:
                        pe.wait_ge(exp_done, n - 1)
                    for k in range(2):
                        head = u % GROUPS * HG + 2 * half + k
                        ins = nc.tensor.matmul(scT[n % 2][:, k, 0:QUERIES - off], kT[:, head, j * P:(j + 1) * P],
                                               qT[s % 2][:, head, off:QUERIES], start=True, stop=True, skip_group_check=True)
                        if is_diagonal(u, j):
                            ins = nc.tensor.matmul(scT[n % 2][:, k, 0:P], ident16[:, :], later16[:, :], start=False, stop=True,
                                                   skip_group_check=True)
                    ins.then_inc(scT_made, 1)

            def attn_v(b):
                u, j = STEPS[b]
                off = first_query(u, j)
                pe.wait_ge(exp_done, 2 * b + 2)
                if j == 0 and u:
                    pe.wait_ge(y_kept, u)
                for h in range(HG):
                    head = u % GROUPS * HG + h
                    ins = nc.tensor.matmul(acc[32 * h:32 * h + VC, off:QUERIES], v[:, j, head, :],
                                           probs[(2 * b + h // 2) % PRING][:, h % 2, 0:QUERIES - off],
                                           start=(j == 0), stop=(j == unit_steps(u) - 1), skip_group_check=True)
                ins.then_inc(pv_done, 1)

            pe.wait_ge(kq_r1, 2 * SUPERS)
            for i in range(ITEMS_BEFORE[1]):
                scores_for_max(i)
            pe.wait_ge(s_const, 9)
            turn_max(0, ms[:, :]).then_inc(w_made, 1)
            pe.wait_ge(v_kept, SUPERS)
            pe.wait_ge(s_const_v, 2)
            pe.wait_ge(maxT_kept, 1)

            def task(name, arg):
                t = (name, arg)
                if name not in CONSUMER:
                    return
                take_bank(pe, t)
                bank = turn_bank(t)
                if name == "max_turn":
                    ins = turn_max(arg, bank)
                if name == "y_turn":
                    s, q = divmod(arg, QT)
                    pe.wait_ge(y_kept, GROUPS * (s + 1))
                    for g in range(GROUPS):
                        ins = nc.tensor.transpose(bank[:, g * P:(g + 1) * P], yT[g][:, q * P:(q + 1) * P], ident[:, :])
                if name == "x1_turn":
                    pe.wait_ge(x1_done, arg + 1)
                    for q in range(QT):
                        ins = nc.tensor.transpose(bank[:, q * P:(q + 1) * P], x1[:, arg * QT + q, :], ident[:, :])
                if name == "logits":
                    pe.wait_ge(empty["scalar"], emptied(TURN[("x1_turn", arg)]))
                    pe.wait_ge(s_router, 16)
                    for q in range(QT):
                        ins = nc.tensor.matmul(bank[:, q * EXPERTS:(q + 1) * EXPERTS], x1T[:, q * P:(q + 1) * P], router[:, :],
                                               start=True, stop=True)
                if name == "count":
                    pe.wait_ge(mask_done, arg + 1)
                    n = 2 * MT
                    counts = bank[:, 0:n * EXPERTS].rearrange("p (n e) -> p n e", e=EXPERTS)
                    nc.tensor.matmul(counts, tri16[:, :], mask16[:, :, :], start=True, stop=False, skip_group_check=True)
                    for i in range(n - 1):
                        ins = nc.tensor.matmul(counts[:, i + 1:n, :], ones16[:, :], mask16[:, i:i + 1, :].to_broadcast([P, n - 1 - i, EXPERTS]),
                                               start=False, stop=(i == n - 2), skip_group_check=True)
                if name == "in_turn":
                    g, part = arg
                    pe.wait_ge(ein_in, 16 * (g + 1))
                    for i in range((QT, 1)[part]):
                        ins = nc.tensor.transpose(bank[:, i * P:(i + 1) * P], ein[:, part * QT + i, :], ident[:, :])
                if name == "expert_h":
                    g, e = arg
                    pe.wait_ge(empty["scalar"], emptied(TURN[("in_turn", (g, 1))]))
                    pe.wait_ge(s_ffw, 32)
                    for f in range(FC):
                        ins = nc.tensor.matmul(bank[:, f * CAP:(f + 1) * CAP], wi[:, e, f * P:(f + 1) * P],
                                               einT[:, e * CAP:(e + 1) * CAP], start=True, stop=True)
                if name == "expert_o":
                    g, e = arg
                    pe.wait_ge(empty["scalar"], emptied(TURN[("expert_h", arg)]))
                    for f in range(FC):
                        ins = nc.tensor.matmul(bank[0:CAP, 0:C], hT[e % 2][:, f, :], wo2[:, e, f, :], start=(f == 0), stop=(f == FC - 1))
                ins.then_inc(turn_made, 1)

            for b in range(LAST + 1):
                if b < NSTEP:
                    for i in WOVEN[b]:
                        scores_for_max(i)
                    scores(b)
                if b >= NSTEP:
                    pe.wait_ge(exp_done, 2 * NSTEP)
                for t in TASKS[b]:
                    if b < NSTEP + LAG:
                        task(*t)
                if LAG <= b < NSTEP + LAG:
                    attn_v(b - LAG)
                if b >= NSTEP + LAG:
                    for t in TASKS[b]:
                        task(*t)


NAMES = ["L0_attn_x", "L0_attn_W_dq", "L0_attn_W_uq", "L0_attn_W_dkv", "L0_attn_W_uk", "L0_attn_W_uv", "L0_attn_W_o",
         "L0_ffn_w_router", "L0_ffn_wi", "L0_ffn_wo"]


def kernel(**inputs):
    import concourse.bacc as bacc
    from concourse.bass_utils import run_bass_kernel_spmd

    nc = bacc.Bacc("TRN2", target_bir_lowering=False, num_devices=1)
    arrays, args = {}, []
    for name in NAMES:
        a = np.ascontiguousarray(inputs[name])
        if name == "L0_attn_x":
            a = a.reshape(T, C)
        arrays[f"in_{name}"] = a
        args.append(nc.dram_tensor(f"in_{name}", a.shape, mybir.dt.from_np(a.dtype), kind="ExternalInput").ap())
    out = nc.dram_tensor("out_y", (T, C), F32, kind="ExternalOutput").ap()
    program(nc, *args, out)
    r = run_bass_kernel_spmd(nc, [arrays], core_ids=[0])
    return np.asarray(r.results[0]["out_y"]).reshape(1, T, C)
```

```python
from contextlib import ExitStack

import numpy as np

import concourse.bass as bass
from concourse import mybir

P = 128
T, C = 2048, 128
HEADS, HD = 16, 8
LAT = 64
QUERIES = 512
SUPERS = T // QUERIES
TILES = T // P
QT = QUERIES // P
HG = 4
GROUPS = HEADS // HG
UNITS = SUPERS * GROUPS
PARTS = 3
COPIES = (PARTS + 2, PARTS)
SPLITS = 3
STORES = (2, 1)
MROW = 126
VC = HD + 1
PRING = 12
SRING = 3
AHEAD = 2
LAG = 2
BIG = -1e38

EXPERTS, FF, CAP = 8, 512, 80
MOE_GROUPS = 2
MT = TILES // MOE_GROUPS
SLOTS = EXPERTS * CAP
ZERO_ROW = SLOTS
TRASH = SLOTS + 1
IN_ROWS = TRASH + 2 * MT * P
FC = FF // P
ST = SLOTS // P
EPS = 1e-5

F32, BF16, U32 = mybir.dt.float32, mybir.dt.bfloat16, mybir.dt.uint32
ALU = mybir.AluOpType
ACT = mybir.ActivationFunctionType
AX = mybir.AxisListType


def super_of(u):
    return u // GROUPS


def unit_steps(u):
    return QT * (super_of(u) + 1)


STEPS = [(u, j) for u in range(UNITS) for j in range(unit_steps(u))]
FIRST = [sum(unit_steps(v) for v in range(u)) for u in range(UNITS + 1)]
NSTEP = len(STEPS)


def first_query(u, j):
    return P * max(0, j - QT * super_of(u))


def is_diagonal(u, j):
    return j >= QT * super_of(u)


def max_items(u):
    return [(qt, h, c) for qt in range(QT) for h in range(HG) for c in range(super_of(u) + 1)]


ITEMS_BEFORE = [0]
for _u in range(UNITS):
    ITEMS_BEFORE.append(ITEMS_BEFORE[-1] + len(max_items(_u)))


def woven():
    out = [[[], [], [], []] for _ in STEPS]
    for u in range(UNITS - AHEAD):
        n, gaps = ITEMS_BEFORE[u + AHEAD + 1] - ITEMS_BEFORE[u + AHEAD], 4 * (unit_steps(u) - 1)
        for i in range(n):
            gap = i * gaps // n
            out[FIRST[u] + gap // 4][gap % 4].append(ITEMS_BEFORE[u + AHEAD] + i)
    return out


WOVEN = woven()
ALL_ITEMS = [(u, *it) for u in range(UNITS) for it in max_items(u)]


def schedule():
    out = []
    for u in range(UNITS - AHEAD):
        out.append((FIRST[u + 1] - 2, "max_rows", u + AHEAD))
        out.append((FIRST[u + 1] - 1, "max_turn", u + AHEAD))
    for u in range(UNITS):
        out.append((FIRST[u + 1] - 1 + LAG, "keep_y", u))
    for s in range(SUPERS):
        b = FIRST[GROUPS * (s + 1)] + 3
        for q in range(QT):
            out.append((b + q, "y_turn", QT * s + q))
        out += [(b + 4, "norm_ln", ("attn", s)), (b + 5, "norm_out", ("attn", s)), (b + 6, "x1_turn", s), (b + 7, "logits", s)]
    for g in range(MOE_GROUPS):
        b = FIRST[2 * GROUPS * (g + 1)] + 3 + 8
        out += [(b, "top2", g), (b + 1, "count", g), (b + 1, "slots", g)]
        b += 9 if g == 0 else 2
        out += [(b, "in_turn", (g, 0)), (b, "in_turn", (g, 1))]
        for e in range(EXPERTS):
            out += [(b + 1 + 2 * e, "expert_h", (g, e)), (b + 2 + 2 * e, "expert_o", (g, e))]
        b += 2 * EXPERTS + 1
        out.append((b, "send_back", g))
        b += 8 if g == 0 else 1
        for half in range(2):
            out += [(b, "combine", (g, half)), (b + 1, "norm_ln", ("moe", 2 * g + half)), (b + 2, "norm_out", ("moe", 2 * g + half))]
            b += 3
    return sorted(out, key=lambda x: x[0])


SCHEDULE = schedule()
LAST = max(x[0] for x in SCHEDULE)
TASKS = [[x[1:] for x in SCHEDULE if x[0] == b] for b in range(LAST + 1)]
ORDERED = [x for b in TASKS for x in b]

CONSUMER = {"max_turn": "vector", "y_turn": "vector", "x1_turn": "scalar", "logits": "vector", "count": "vector",
            "in_turn": "scalar", "expert_h": "scalar", "expert_o": "vector"}
TURNS = [x for x in ORDERED if x[0] in CONSUMER]
TURN = {x: n for n, x in enumerate(TURNS)}
TAIL_TURN = sum(1 for b in TASKS[:NSTEP + LAG] for x in b if x[0] in CONSUMER)
TAIL_BANKS = (7, 0, 1, 2, 3, 4, 5)


def bank_of(n):
    return 7 if n < TAIL_TURN else TAIL_BANKS[(n - TAIL_TURN) % len(TAIL_BANKS)]


def emptied(n):
    return sum(1 for m in range(n + 1) if CONSUMER[TURNS[m][0]] == CONSUMER[TURNS[n][0]])


def norm_count(key):
    return [x[1] for x in ORDERED if x[0] == "norm_ln"].index(key) + 1


def program(nc, x_d, wdq_d, wuq_d, wdkv_d, wuk_d, wuv_d, wo_d, router_d, wi_d, wo2_d, out_d):
    ctx = ExitStack()
    with ctx:
        def sb(name, shape, dt=F32):
            return ctx.enter_context(nc.sbuf_tensor(name, shape, dt))

        def sem(name):
            return ctx.enter_context(nc.semaphore(name))

        parts_d = [nc.dram_tensor(f"parts_{n}", (COPIES[i], C, T), BF16, kind="Internal").ap() for i, n in enumerate("kq")]
        exp_in_d = [nc.dram_tensor(f"exp_in_{g}", (IN_ROWS, C), F32, kind="Internal").ap() for g in range(MOE_GROUPS)]
        exp_out_d = [nc.dram_tensor(f"exp_out_{g}", (SLOTS + 1, C), F32, kind="Internal").ap() for g in range(MOE_GROUPS)]

        kT = sb("kT", [P, HEADS, T], BF16)
        qT = [sb(f"qT{i}", [P, HEADS, QUERIES], BF16) for i in range(2)]
        v = sb("v", [P, TILES, HEADS, VC])
        probs = [sb(f"probs{i}", [P, QUERIES]) for i in range(PRING)]
        x = sb("x", [P, TILES, C])
        x1 = sb("x1", [P, TILES, C])
        yT = [sb(f"yT{g}", [P, QUERIES]) for g in range(GROUPS)]
        wi = sb("wi", [P, EXPERTS, FF])
        wo2 = sb("wo2", [P, EXPERTS, FC, C])
        xT = wo2[:, :, :, :].rearrange("p e f c -> p (e f c)")[:, 0:T]
        wi_flat = wi[:, :, :].rearrange("p e f -> p (e f)")
        rest = [wi_flat[:, i * QUERIES:(i + 1) * QUERIES] for i in range(2)]
        split = [wi_flat[:, 1024 + i * 768:1024 + (i + 1) * 768].bitcast(BF16).rearrange("p (a t) -> p a t", a=PARTS)
                 for i in range(4)]
        x1_flat = x1[:, :, :].rearrange("p n c -> p (n c)")
        split += [x1_flat[:, i * 768:(i + 1) * 768].bitcast(BF16).rearrange("p (a t) -> p a t", a=PARTS) for i in range(2)]

        router = sb("router", [C, EXPERTS])
        small = wo2[:, :, :, :].rearrange("p e f c -> p (e f c)")[:, T:2 * T]

        def early(i, rows, cols):
            return small[0:rows, i * C:i * C + cols]

        wdq, wuq, wdkv, wuk = early(0, LAT, C), early(1, C, LAT), early(2, LAT, C), early(3, C, LAT)
        wuv, wo, wuqT, woT = early(4, C, LAT), early(5, C, C), early(6, LAT, C), early(7, C, C)
        uq_uk, keffT, veff = early(8, LAT, LAT), early(9, LAT, C), early(10, LAT, C)
        qw, kw, vw = early(11, C, C), early(12, C, C), early(13, C, C)

        ident = sb("ident", [P, P])
        ident16 = sb("ident16", [P, P], BF16)
        ones16 = sb("ones16", [P, P], BF16)
        tri16 = sb("tri16", [P, P], BF16)
        later16 = sb("later16", [P, P], BF16)
        causal = sb("causal", [P, QUERIES])
        iota_e = sb("iota_e", [P, EXPERTS])
        trash1 = sb("trash1", [P, 2 * MT])

        unused = [sb(f"unused{i}", [P, QUERIES], BF16) for i in range(2)]
        part_max = [sb(f"part_max{i}", [P, QT * HG, SUPERS]) for i in range(2)]
        neg_max = sb("neg_max", [P, QT * HG])
        max16 = [sb(f"max16_{i}", [P, QT, 2, HG], BF16) for i in range(2)]
        maxT = [sb(f"maxT{i}", [2 * HG, QUERIES], BF16) for i in range(2)]

        recip = sb("recip", [P, HEADS, 1])
        res = sb("res", [P, QT, C])
        stats = sb("stats", [P, QT, 6])
        mv = sb("mv", [P, QT, 2])
        var = sb("var", [P, QT])
        lnv = sb("lnv", [P, QT])
        rs0 = sb("rs0", [P, QT])
        rs = sb("rs", [P, QT])
        nt = sb("nt", [P, QT])
        lg = sb("lg", [P, MT, EXPERTS])
        top = sb("top", [P, MT, 8])
        top_i = sb("top_i", [P, MT, 8], U32)
        expert = sb("expert", [P, 2, MT])
        mask16 = sb("mask16", [P, 2 * MT, EXPERTS], BF16)
        lgm = sb("lgm", [P, MT, 8])
        ex = sb("ex", [P, MT, 8])
        exs = sb("exs", [P, MT])
        exr = sb("exr", [P, MT])
        gate = sb("gate", [P, 2, MT])
        cw = sb("cw", [P, 2 * MT, EXPERTS])
        place = sb("place", [P, 2 * MT])
        slot = sb("slot", [P, 2 * MT])
        over = sb("over", [P, 2 * MT])
        away = sb("away", [P, 2 * MT])
        slot_in = sb("slot_in", [P, 2 * MT], U32)
        slot_out = sb("slot_out", [P, 2 * MT], U32)
        einT = sb("einT", [P, SLOTS])
        x1T = einT[:, 0:QUERIES]
        hT = [sb(f"hT{i}", [P, FC, CAP]) for i in range(2)]
        back2 = sb("back2", [P, MT, C])
        ein = back2[:, 0:ST, :]

        scT = [ctx.enter_context(nc.psum_tensor(f"scT{i}", [P, QUERIES], F32)) for i in range(SRING)]
        sc = [ctx.enter_context(nc.psum_tensor(f"sc{i}", [P, QUERIES], F32)) for i in range(SRING)]
        acc = ctx.enter_context(nc.psum_tensor("acc", [P, QUERIES], F32))
        ms = ctx.enter_context(nc.psum_tensor("ms", [P, QUERIES], F32))
        BANKS = [t[:, :] for t in (*scT, *sc, acc, ms)]

        s_w = sem("s_w")
        s_router = sem("s_router")
        s_x = [sem(f"s_x{i}") for i in range(SUPERS)]
        s_ffw = sem("s_ffw")
        s_const = sem("s_const")
        s_const_v = sem("s_const_v")
        s_rows = sem("s_rows")
        q_rows = sem("q_rows")
        q_rows0 = sem("q_rows0")
        w_made = sem("w_made")
        w_kept = sem("w_kept")
        xT_made = sem("xT_made")
        xT_kept = sem("xT_kept")
        kq_made = sem("kq_made")
        kq_hi = sem("kq_hi")
        kq_r1 = sem("kq_r1")
        kq_mid = sem("kq_mid")
        kq_lo = sem("kq_lo")
        parts_out = [sem(f"parts_out{i}") for i in range(2 * SPLITS)]
        v_made = sem("v_made")
        v_kept = sem("v_kept")
        kq_in = [sem(f"kq_in{i}") for i in range(SUPERS)]
        sc_made = sem("sc_made")
        sc_used = sem("sc_used")
        max_done = sem("max_done")
        maxT_kept = sem("maxT_kept")
        max_in = [sem(f"max_in{i}") for i in range(2)]
        scT_made = sem("scT_made")
        exp_done = sem("exp_done")
        pv_done = sem("pv_done")
        y_kept = sem("y_kept")
        turn_made = sem("turn_made")
        empty = {"vector": sem("empty_v"), "scalar": sem("empty_s")}
        var_ready = sem("var_ready")
        rs_ready = sem("rs_ready")
        x1_done = sem("x1_done")
        lgm_done = sem("lgm_done")
        ex_done = sem("ex_done")
        mask_done = sem("mask_done")
        slots_done = sem("slots_done")
        cleared = sem("cleared")
        scattered = [sem(f"scattered{g}") for g in range(MOE_GROUPS)]
        ein_in = sem("ein_in")
        o_kept = sem("o_kept")
        o_out = sem("o_out")
        gathered = [sem(f"gathered{g}") for g in range(MOE_GROUPS)]
        out_ready = sem("out_ready")
        s_out = sem("s_out")
        chain = sem("chain")

        def turn_bank(task):
            return BANKS[bank_of(TURN[task])]

        def take_bank(eng, task):
            n = TURN[task]
            before = [m for m in range(n) if bank_of(m) == bank_of(n)]
            if before:
                eng.wait_ge(empty[CONSUMER[TURNS[before[-1]][0]]], emptied(before[-1]))

        def kq_banks(i):
            return (sc[0], sc[1]) if i % 2 == 0 else (acc, ms)

        def token_rows(d, a, b):
            return d[a * P:b * P, :].rearrange("(n p) c -> p n c", p=P)

        block = ctx.enter_context(nc.Block())

        @block.sync
        def _(sp):
            for dst, src in ((wuq, wuq_d), (wuk, wuk_d), (wo, wo_d), (wdq, wdq_d), (wuv, wuv_d), (wdkv, wdkv_d)):
                sp.dma_start(dst, src).then_inc(s_w, 16)
            for i in range(SUPERS):
                sp.dma_start(x[:, i * QT:(i + 1) * QT, :], token_rows(x_d, i * QT, (i + 1) * QT)).then_inc(s_x[i], 16)
            sp.dma_start(router[:, :], router_d).then_inc(s_router, 16)
            sp.wait_ge(s_const, 3)
            for g in range(MOE_GROUPS):
                sp.dma_start(exp_in_d[g][0:SLOTS, :].rearrange("(n p) c -> p n c", p=P),
                             causal[:, 0:C].unsqueeze(1).to_broadcast([P, ST, C])).then_inc(cleared, 16)
                sp.dma_start(exp_out_d[g][ZERO_ROW:ZERO_ROW + 1, :], causal[0:1, 0:C]).then_inc(cleared, 16)

            def store_parts(i, n):
                sp.wait_ge(kq_mid, 2 * i + n + 1)
                sp.wait_ge(kq_lo, 2 * i + n + 1)
                for first in range(0, COPIES[n], PARTS):
                    count = min(PARTS, COPIES[n] - first)
                    sp.dma_start(parts_d[n].rearrange("b c t -> c b t")[:, first:first + count, i * QUERIES:(i + 1) * QUERIES],
                                 split[2 * (i % SPLITS) + n][:, 0:count, :]).then_inc(parts_out[2 * (i % SPLITS) + n], 16)

            def load_products(n, a, b, done):
                rows = PARTS * HD
                all_rows = parts_d[n].rearrange("b (d h) t -> (b d) h t", h=HEADS)
                dst = kT[:, :, a * QUERIES:b * QUERIES] if n == 0 else qT[a % 2][:, :, :]
                for turn in range(PARTS):
                    first = turn * HD if n == 0 else 0
                    sp.dma_start(dst[turn * rows:(turn + 1) * rows, :, :],
                                 all_rows[first:first + rows, :, a * QUERIES:b * QUERIES]).then_inc(done, 16)

            def max_to_rows(u):
                sp.wait_ge(maxT_kept, u + 1)
                q, g = qT[super_of(u) % 2], u % GROUPS
                for part in range(2):
                    sp.dma_start(q[MROW + part:MROW + part + 1, g * HG:(g + 1) * HG, :],
                                 maxT[u % 2][part * HG:(part + 1) * HG, :]).then_inc(max_in[u % 2], 16)

            for i in range(SUPERS):
                for n in range(2):
                    store_parts(i, n)
                if i < 2:
                    for n in range(2):
                        sp.wait_ge(*((s_rows, i + 1) if n == 0 else ((q_rows0, q_rows)[i], 1)))
                        sp.wait_ge(parts_out[2 * i + n], 16 * STORES[n])
                        load_products(n, i, i + 1, kq_in[i])
            for u in range(AHEAD):
                max_to_rows(u)
            sp.wait_ge(s_rows, SUPERS)
            for i in range(2, SUPERS):
                sp.wait_ge(parts_out[2 * (i % SPLITS)], 16 * STORES[0] * (i // SPLITS + 1))
                load_products(0, i, i + 1, kq_in[i])
            for b in range(LAST + 1):
                if b == FIRST[GROUPS]:
                    for i in range(SUPERS):
                        sp.wait_ge(parts_out[2 * (i % SPLITS) + 1], 16 * STORES[1] * (i // SPLITS + 1))
                    sp.wait_ge(v_made, SUPERS)
                    sp.dma_start(wi[:, :, :], wi_d.rearrange("e h f -> h e f")).then_inc(s_ffw, 16)
                    sp.dma_start(wo2[:, :, :, :], wo2_d.rearrange("e (f p) h -> p e f h", p=P)).then_inc(s_ffw, 16)
                for name, arg in TASKS[b]:
                    if name == "max_turn":
                        max_to_rows(arg)
                        if arg in (GROUPS + AHEAD, 2 * GROUPS + AHEAD):
                            s = super_of(arg) + 1
                            sp.wait_ge(scT_made, HG * FIRST[GROUPS * (s - 1)])
                            load_products(1, s, s + 1, kq_in[s])
                    if name == "expert_o" and arg[1] in (EXPERTS // 2 - 1, EXPERTS - 1):
                        g, e = arg
                        e0 = e + 1 - EXPERTS // 2
                        sp.wait_ge(o_kept, EXPERTS * g + e + 1)
                        sp.dma_start(exp_out_d[g][e0 * CAP:(e + 1) * CAP, :].rearrange("(e p) h -> p e h", p=CAP),
                                     x[0:CAP, g * MT + e0:g * MT + e + 1, :]).then_inc(o_out, 16)
                    if name == "slots":
                        sp.wait_ge(scattered[arg], 16 * 2 * MT)
                        if arg:
                            sp.wait_ge(out_ready, 2 * arg)
                        sp.dma_start(ein, exp_in_d[arg][0:SLOTS, :].rearrange("(n p) c -> p n c", p=P)).then_inc(ein_in, 16)
                    if name == "norm_out" and arg[0] == "moe":
                        k = arg[1]
                        sp.wait_ge(out_ready, k + 1)
                        sp.dma_start(token_rows(out_d, k * QT, (k + 1) * QT),
                                     x[:, k * QT:(k + 1) * QT, :]).then_inc(s_out, 16)
            sp.wait_ge(s_out, 16 * SUPERS)

        @block.gpsimd
        def _(pool):
            nc.gpsimd.memset(ident[:, :], 0.0).then_inc(s_const, 1)
            nc.gpsimd.memset(ones16[:, :], 1.0).then_inc(s_const, 1)
            nc.gpsimd.memset(causal[:, :], 0.0).then_inc(s_const, 1)
            pool.wait_ge(s_const, 3)
            nc.gpsimd.affine_select(out=ident[:, :], in_=ident[:, :], compare_op=ALU.not_equal, fill=1.0, base=0,
                                    pattern=[[-1, P]], channel_multiplier=1).then_inc(s_const, 1)
            pool.wait_ge(s_const, 4)
            nc.gpsimd.tensor_copy(ident16[:, :], ident[:, :]).then_inc(s_const, 1)
            nc.gpsimd.affine_select(out=tri16[:, :], in_=ones16[:, :], compare_op=ALU.is_ge, fill=0.0, base=0,
                                    pattern=[[1, P]], channel_multiplier=-1).then_inc(s_const, 1)
            nc.gpsimd.memset(later16[:, :], 0.0).then_inc(s_const, 1)
            pool.wait_ge(s_const, 7)
            nc.gpsimd.affine_select(out=later16[:, :], in_=later16[:, :], compare_op=ALU.is_ge, fill=BIG, base=0,
                                    pattern=[[1, P]], channel_multiplier=-1).then_inc(s_const, 1)
            tri = causal[:, QUERIES - P:QUERIES]
            nc.gpsimd.affine_select(out=tri, in_=tri, compare_op=ALU.is_ge, fill=BIG, base=0,
                                    pattern=[[-1, P]], channel_multiplier=1).then_inc(s_const, 1)
            one_pair = 0x3F803F80

            def fill_k(i):
                rows = kT[P // 2:P, :, i * QUERIES:(i + 1) * QUERIES].bitcast(U32)
                nc.gpsimd.memset(rows, one_pair).then_inc(s_rows, 1)

            pool.wait_ge(s_const, 9)
            fill_k(0)
            fill_k(1)
            nc.gpsimd.memset(qT[1][P // 2:P, :, :].bitcast(U32), 0).then_inc(q_rows, 1)
            for i in range(2, SUPERS):
                fill_k(i)
            pool.wait_ge(s_rows, SUPERS)
            pool.wait_ge(q_rows, 1)
            nc.gpsimd.iota(iota_e[:, :], [[1, EXPERTS]], base=0, channel_multiplier=0,
                           allow_small_or_imprecise_dtypes=True).then_inc(s_const, 1)
            nc.gpsimd.iota(trash1[:, :], [[P, 2 * MT]], base=TRASH + 1, channel_multiplier=1,
                           allow_small_or_imprecise_dtypes=True).then_inc(s_const, 1)

            def scatter(g):
                pool.wait_ge(slots_done, g + 1)
                pool.wait_ge(cleared, 16 * 4)
                for n in range(2 * MT):
                    pool.indirect_dma_start(exp_in_d[g][:, :], bass.IndirectOffsetOnAxis(slot_in[:, n:n + 1], 0),
                                            x1[:, g * MT + n % MT, :], None).then_inc(scattered[g], 16)

            def gather(g):
                pool.wait_ge(o_out, 16 * 2 * (g + 1))
                for n in range(2 * MT):
                    dst = x[:, g * MT + n, :] if n < MT else back2[:, n - MT, :]
                    pool.indirect_dma_start(dst, None, exp_out_d[g][:, :],
                                            bass.IndirectOffsetOnAxis(slot_out[:, n:n + 1], 0)).then_inc(gathered[g], 16)

            for b in range(LAST + 1):
                for name, arg in TASKS[b]:
                    if name == "slots":
                        scatter(arg)
                    if name == "send_back":
                        gather(arg)

        @block.scalar
        def _(act):
            nc.scalar.preload_act_table_set("natural_log_exp_and_others")
            for i in range(SUPERS):
                for n in range(2):
                    k = 2 * i + n
                    act.wait_ge(kq_made, k + 1)
                    if i >= SPLITS:
                        act.wait_ge(parts_out[2 * (i % SPLITS) + n], 16 * STORES[n])
                    nc.scalar.activation(split[2 * (i % SPLITS) + n][:, 0, :], kq_banks(i)[n][:, :], ACT.Copy).then_inc(kq_hi, 1)
                for n in range(2):
                    k = 2 * i + n
                    act.wait_ge(kq_r1, k + 1)
                    nc.scalar.activation(split[2 * (i % SPLITS) + n][:, 1, :], rest[n], ACT.Copy).then_inc(kq_mid, 1)
                act.wait_ge(v_made, i + 1)
                act.wait_ge(s_const_v, 1)
                nc.scalar.activation(v[:, i * QT:(i + 1) * QT, :, 0:HD],
                                     scT[2][:, :].rearrange("p (n h d) -> p n h d", n=QT, h=HEADS), ACT.Copy).then_inc(v_kept, 1)

            def exps(b):
                u, j = STEPS[b]
                width = QUERIES - first_query(u, j)
                for n in range(HG * b, HG * b + HG):
                    act.wait_ge(scT_made, n + 1)
                    if n >= PRING:
                        act.wait_ge(pv_done, (n - PRING) // HG + 1)
                    nc.scalar.activation(probs[n % PRING][:, 0:width], scT[n % SRING][:, 0:width], ACT.Exp).then_inc(exp_done, 1)

            for b in range(LAST + 1):
                if b < NSTEP:
                    exps(b)
                for name, arg in TASKS[b]:
                    if name == "keep_y":
                        act.wait_ge(pv_done, FIRST[arg + 1])
                        if arg >= GROUPS:
                            act.wait_ge(turn_made, TURN[("y_turn", QT * super_of(arg) - 1)] + 1)
                        nc.scalar.activation(yT[arg % GROUPS][:, :], acc[:, :], ACT.Copy).then_inc(y_kept, 1)
                    if name == "norm_ln":
                        k = norm_count(arg)
                        act.wait_ge(var_ready, k)
                        nc.scalar.activation(lnv[:, :], var[:, :], ACT.Ln).then_inc(rs_ready, 1)
                        act.wait_ge(rs_ready, 2 * k - 1)
                        nc.scalar.activation(rs0[:, :], lnv[:, :], ACT.Exp, scale=-0.5).then_inc(rs_ready, 1)
                    if name == "x1_turn":
                        act.wait_ge(turn_made, TURN[(name, arg)] + 1)
                        if arg:
                            last = ("expert_h", (arg // 2 - 1, EXPERTS - 1)) if arg % 2 == 0 else ("logits", arg - 1)
                            act.wait_ge(turn_made, TURN[last] + 1)
                        nc.scalar.activation(x1T, turn_bank((name, arg)), ACT.Copy).then_inc(empty["scalar"], 1)
                    if name == "top2":
                        act.wait_ge(lgm_done, arg + 1)
                        nc.scalar.activation(ex[:, :, :], lgm[:, :, :], ACT.Exp).then_inc(ex_done, 1)
                    if name == "in_turn":
                        act.wait_ge(turn_made, TURN[(name, arg)] + 1)
                        act.wait_ge(turn_made, TURN[("logits", 2 * arg[0] + 1)] + 1)
                        n = (QT, 1)[arg[1]] * P
                        nc.scalar.activation(einT[:, arg[1] * QUERIES:arg[1] * QUERIES + n], turn_bank((name, arg))[:, 0:n],
                                             ACT.Copy).then_inc(empty["scalar"], 1)
                    if name == "expert_h":
                        act.wait_ge(turn_made, TURN[(name, arg)] + 1)
                        if arg[0] * EXPERTS + arg[1] >= 2:
                            e = arg[0] * EXPERTS + arg[1] - 2
                            act.wait_ge(turn_made, TURN[("expert_o", (e // EXPERTS, e % EXPERTS))] + 1)
                        nc.scalar.activation(hT[arg[1] % 2][:, :, :], turn_bank((name, arg))[:, 0:FC * CAP].rearrange("p (f t) -> p f t", f=FC),
                                             ACT.Relu).then_inc(empty["scalar"], 1)

        @block.vector
        def _(dve):
            made = [0]

            def link(ins):
                made[0] += 1
                ins.then_inc(chain, 1)
                dve.wait_ge(chain, made[0])

            nc.vector.memset(v[:, :, :, HD:VC], 1.0).then_inc(s_const_v, 1)
            nc.vector.memset(qT[0][P // 2:P, :, :].bitcast(U32), 0).then_inc(q_rows0, 1)
            def by_value(w):
                return w.rearrange("p (h d) -> p d h", d=HD)

            dve.wait_ge(w_made, 1)
            nc.vector.tensor_copy(wuqT, sc[0][0:LAT, 0:C]).then_inc(w_kept, 1)
            nc.vector.tensor_copy(woT, sc[0][:, C:2 * C]).then_inc(w_kept, 1)
            nc.vector.tensor_copy(uq_uk, sc[1][0:LAT, 0:LAT]).then_inc(w_kept, 1)
            dve.wait_ge(w_made, 2)
            nc.vector.tensor_scalar(qw.rearrange("p (d h) -> p d h", h=HEADS), by_value(acc[:, 0:C]), float(HD) ** -0.5, None, ALU.mult).then_inc(w_kept, 1)
            nc.vector.tensor_copy(keffT, ms[0:LAT, 0:C]).then_inc(w_kept, 1)
            nc.vector.tensor_copy(veff, ms[0:LAT, C:2 * C]).then_inc(w_kept, 1)
            dve.wait_ge(w_made, 3)
            nc.vector.tensor_copy(kw.rearrange("p (d h) -> p d h", h=HEADS), by_value(sc[2][:, 0:C])).then_inc(w_kept, 1)
            nc.vector.tensor_copy(vw, sc[2][:, C:2 * C]).then_inc(w_kept, 1)
            def keep_xT(i):
                dve.wait_ge(xT_made, i + 1)
                nc.vector.tensor_copy(xT[:, i * QUERIES:(i + 1) * QUERIES], scT[i % 2][:, :]).then_inc(xT_kept, 1)

            keep_xT(0)
            for i in range(SUPERS):
                if i + 1 < SUPERS:
                    keep_xT(i + 1)
                parts = split[2 * (i % SPLITS):2 * (i % SPLITS) + 2]
                for n in range(2):
                    dve.wait_ge(kq_hi, 2 * i + n + 1)
                    if i:
                        dve.wait_ge(kq_lo, 2 * (i - 1) + n + 1)
                    nc.vector.tensor_tensor(rest[n], kq_banks(i)[n][:, :], parts[n][:, 0, :], ALU.subtract).then_inc(kq_r1, 1)
                for n in range(2):
                    dve.wait_ge(kq_mid, 2 * i + n + 1)
                    nc.vector.tensor_tensor(parts[n][:, 2, :], rest[n], parts[n][:, 1, :], ALU.subtract).then_inc(kq_lo, 1)

            dve.wait_ge(kq_r1, 2 * SUPERS)
            nc.vector.memset(acc[:, :], 0.0).then_inc(s_const_v, 1)

            def row_max(i):
                u, qt, h, c = ALL_ITEMS[i]
                dve.wait_ge(sc_made, i + 1)
                dst = part_max[u % 2][:, qt * HG + h, c:c + 1]
                if c < super_of(u):
                    nc.vector.tensor_reduce(dst, sc[i % SRING][:, :], AX.X, ALU.max).then_inc(sc_used, 1)
                else:
                    w = (qt + 1) * P
                    if i >= 2:
                        dve.wait_ge(sc_used, i - 1)
                    nc.vector.tensor_tensor_reduce(unused[i % 2][:, 0:w], sc[i % SRING][:, 0:w], causal[:, QUERIES - w:QUERIES], 1.0, 3 * BIG,
                                                   ALU.add, ALU.max, dst).then_inc(sc_used, 1)

            def max_rows(u):
                dve.wait_ge(sc_used, ITEMS_BEFORE[u + 1])
                if u >= 2:
                    if u < 2 + AHEAD:
                        dve.wait_ge(w_made, 4 + u - 2)
                    else:
                        dve.wait_ge(turn_made, TURN[("max_turn", u - 2)] + 1)
                link(nc.vector.tensor_reduce(neg_max[:, :], part_max[u % 2][:, :, 0:super_of(u) + 1], AX.X, ALU.max, negate=True))
                m = max16[u % 2]
                nm = neg_max[:, :].rearrange("p (q h) -> p q h", q=QT)
                link(nc.vector.tensor_copy(m[:, :, 0, :], nm))
                nc.vector.tensor_tensor(m[:, :, 1, :], nm, m[:, :, 0, :], ALU.subtract).then_inc(max_done, 1)

            def keep_maxT(u, bank):
                if u >= 2:
                    dve.wait_ge(max_in[u % 2], 32 * (u // 2))
                return nc.vector.tensor_copy(maxT[u % 2][:, :], bank.bitcast(BF16)[0:2 * HG, 0:QUERIES])

            dve.wait_ge(s_const, 11)
            for u in range(AHEAD):
                for i in range(ITEMS_BEFORE[u], ITEMS_BEFORE[u + 1]):
                    row_max(i)
                max_rows(u)
                dve.wait_ge(w_made, 4 + u)
                keep_maxT(u, ms[:, :]).then_inc(maxT_kept, 1)

            def y_turn(tile):
                s, q = divmod(tile, QT)
                bank = turn_bank(("y_turn", tile)).rearrange("p (h e) -> p h e", h=HEADS)
                dve.wait_ge(turn_made, TURN[("y_turn", tile)] + 1)
                link(nc.vector.reciprocal(recip[:, :, :], bank[:, :, HD:VC]))
                r = res[:, q, :]
                made[0] += 1
                nc.vector.tensor_tensor(r.rearrange("p (h d) -> p h d", h=HEADS), bank[:, :, 0:HD],
                                        recip[:, :, :].to_broadcast([P, HEADS, HD]), ALU.mult).then_inc(chain, 1)
                dve.wait_ge(chain, made[0])
                nc.vector.sem_inc(empty["vector"], 1)
                link(nc.vector.tensor_tensor(r, r, x[:, tile, :], ALU.add))
                link(nc.vector.bn_stats(stats[:, q, :], r))
                link(nc.vector.bn_aggr(mv[:, q, :], stats[:, q, :]))

            def norm_out(kind, k):
                n = norm_count((kind, k))
                dve.wait_ge(rs_ready, 2 * n)
                link(nc.vector.tensor_tensor(nt[:, :], rs0[:, :], rs0[:, :], ALU.mult))
                link(nc.vector.tensor_tensor(nt[:, :], nt[:, :], var[:, :], ALU.mult))
                link(nc.vector.tensor_scalar(nt[:, :], nt[:, :], -0.5, 1.5, ALU.mult, ALU.add))
                link(nc.vector.tensor_tensor(rs[:, :], rs0[:, :], nt[:, :], ALU.mult))
                if (kind, k) == ("attn", 0):
                    for n in range(2):
                        dve.wait_ge(parts_out[2 * (SPLITS - 1) + n], 16 * STORES[n])
                for q in range(QT):
                    if kind == "attn":
                        src, dst = res[:, q, :], x1[:, k * QT + q, :]
                    else:
                        src = dst = x[:, k * QT + q, :]
                    ins = nc.vector.tensor_scalar(dst, src, mv[:, q, 0:1], rs[:, q:q + 1], ALU.subtract, ALU.mult)
                    if q == QT - 1:
                        ins.then_inc(x1_done if kind == "attn" else out_ready, 1)

            def top2(g):
                for i in range(MT):
                    ins = nc.vector.max(top[:, i, :], lg[:, i, :])
                link(ins)
                if g:
                    dve.wait_ge(gathered[g - 1], 16 * 2 * MT)
                for i in range(MT):
                    nc.vector.max_index(top_i[:, i, :], top[:, i, :], lg[:, i, :])
                nc.vector.tensor_tensor(lgm[:, :, :], top[:, :, :], top[:, :, 0:1].to_broadcast([P, MT, 8]),
                                        ALU.subtract).then_inc(lgm_done, 1)
                link(nc.vector.memset(exs[:, :], 0.0))
                link(nc.vector.tensor_copy(expert[:, :, :], top_i[:, :, 0:2].rearrange("p i k -> p k i")))
                nc.vector.tensor_tensor(mask16[:, :, :], iota_e[:, :].unsqueeze(1).to_broadcast([P, 2 * MT, EXPERTS]),
                                        expert[:, :, :].rearrange("p k i -> p (k i)").unsqueeze(2).to_broadcast([P, 2 * MT, EXPERTS]),
                                        ALU.is_equal).then_inc(mask_done, 1)
                dve.wait_ge(ex_done, g + 1)
                link(nc.vector.tensor_reduce(exs[:, :], ex[:, :, :], AX.X, ALU.add))
                link(nc.vector.reciprocal(exr[:, :], exs[:, :]))
                nc.vector.tensor_tensor(gate[:, :, :], ex[:, :, 0:2].rearrange("p i k -> p k i"),
                                        exr[:, :].unsqueeze(1).to_broadcast([P, 2, MT]), ALU.mult).then_inc(chain, 1)
                made[0] += 1

            def slots(g):
                dve.wait_ge(turn_made, TURN[("count", g)] + 1)
                counts = turn_bank(("count", g))[:, 0:2 * MT * EXPERTS].rearrange("p (n e) -> p n e", e=EXPERTS)
                made[0] += 1
                nc.vector.tensor_tensor(cw[:, :, :], counts, mask16[:, :, :], ALU.mult).then_inc(chain, 1)
                dve.wait_ge(chain, made[0])
                nc.vector.sem_inc(empty["vector"], 1)
                link(nc.vector.tensor_reduce(place[:, :], cw[:, :, :], AX.X, ALU.add))
                link(nc.vector.scalar_tensor_tensor(slot[:, :], expert[:, :, :].rearrange("p k i -> p (k i)"), float(CAP), place[:, :],
                                                    ALU.mult, ALU.add))
                link(nc.vector.tensor_scalar(over[:, :], place[:, :], float(CAP), None, ALU.is_gt))
                link(nc.vector.tensor_tensor(away[:, :], trash1[:, :], slot[:, :], ALU.subtract))
                link(nc.vector.tensor_tensor(away[:, :], away[:, :], over[:, :], ALU.mult))
                link(nc.vector.tensor_tensor(slot[:, :], slot[:, :], away[:, :], ALU.add))
                nc.vector.tensor_scalar(slot_out[:, :], slot[:, :], float(ZERO_ROW + 1), -1.0, ALU.min, ALU.add)
                nc.vector.tensor_scalar(slot_in[:, :], slot[:, :], -1.0, None, ALU.add).then_inc(slots_done, 1)

            def combine(g, half):
                dve.wait_ge(gathered[g], 16 * 2 * MT)
                for q in range(QT):
                    i = half * QT + q
                    a, b = x[:, g * MT + i, :], back2[:, i, :]
                    link(nc.vector.scalar_tensor_tensor(a, a, gate[:, 0, i:i + 1], x1[:, g * MT + i, :], ALU.mult, ALU.add))
                    link(nc.vector.scalar_tensor_tensor(a, b, gate[:, 1, i:i + 1], a, ALU.mult, ALU.add))
                    link(nc.vector.bn_stats(stats[:, q, :], a))
                    link(nc.vector.bn_aggr(mv[:, q, :], stats[:, q, :]))

            for b in range(LAST + 1):
                if b < NSTEP:
                    for i in sum(WOVEN[b], []):
                        row_max(i)
                for name, arg in TASKS[b]:
                    if name == "max_rows":
                        max_rows(arg)
                    if name == "max_turn":
                        dve.wait_ge(turn_made, TURN[(name, arg)] + 1)
                        made[0] += 1
                        keep_maxT(arg, turn_bank((name, arg))).then_inc(maxT_kept, 1)
                        dve.wait_ge(maxT_kept, arg + 1)
                        nc.vector.sem_inc(empty["vector"], 1)
                        made[0] -= 1
                    if name == "y_turn":
                        y_turn(arg)
                    if name == "norm_ln":
                        nc.vector.tensor_scalar(var[:, :], mv[:, :, 1], EPS, None, ALU.add).then_inc(var_ready, 1)
                    if name == "norm_out":
                        norm_out(*arg)
                    if name == "logits":
                        dve.wait_ge(turn_made, TURN[(name, arg)] + 1)
                        nc.vector.tensor_copy(lg[:, (arg % 2) * QT:(arg % 2 + 1) * QT, :],
                                              turn_bank((name, arg))[:, 0:QT * EXPERTS].rearrange("p (q e) -> p q e", e=EXPERTS)
                                              ).then_inc(empty["vector"], 1)
                    if name == "top2":
                        dve.wait_ge(empty["vector"], emptied(TURN[("logits", 2 * arg + 1)]))
                        top2(arg)
                    if name == "slots":
                        slots(arg)
                    if name == "expert_o":
                        g, e = arg
                        dve.wait_ge(turn_made, TURN[(name, arg)] + 1)
                        nc.vector.tensor_copy(x[0:CAP, g * MT + e, :], turn_bank((name, arg))[0:CAP, 0:C]).then_inc(o_kept, 1)
                        dve.wait_ge(o_kept, EXPERTS * g + e + 1)
                        nc.vector.sem_inc(empty["vector"], 1)
                    if name == "combine":
                        combine(*arg)

        @block.tensor
        def _(pe):
            pe.wait_ge(s_const, 4)
            pe.wait_ge(s_w, 16 * 6)
            nc.tensor.transpose(sc[0][0:LAT, 0:C], wuq, ident[:, :])
            nc.tensor.transpose(sc[0][:, C:2 * C], wo, ident[:, :])
            nc.tensor.matmul(sc[1][0:LAT, 0:LAT], wuq, wuk, start=True, stop=True).then_inc(w_made, 1)

            def turn_x(i):
                pe.wait_ge(s_x[i], 16)
                if i >= 2:
                    pe.wait_ge(xT_kept, i - 1)
                for q in range(QT):
                    ins = nc.tensor.transpose(scT[i % 2][:, q * P:(q + 1) * P], x[:, i * QT + q, :], ident[:, :])
                ins.then_inc(xT_made, 1)

            turn_x(0)
            pe.wait_ge(w_kept, 3)
            nc.tensor.matmul(acc[:, 0:C], wdq, wuqT, start=True, stop=True)
            nc.tensor.matmul(ms[0:LAT, 0:C], uq_uk, wdq, start=True, stop=True)
            nc.tensor.matmul(ms[0:LAT, C:2 * C], wuv, woT, start=True, stop=True).then_inc(w_made, 1)
            turn_x(1)
            pe.wait_ge(w_kept, 6)
            nc.tensor.matmul(sc[2][:, 0:C], wdkv, keffT, start=True, stop=True)
            nc.tensor.matmul(sc[2][:, C:2 * C], wdkv, veff, start=True, stop=True).then_inc(w_made, 1)
            pe.wait_ge(w_kept, 8)
            for i in range(SUPERS):
                pe.wait_ge(xT_kept, i + 1)
                xt = xT[:, i * QUERIES:(i + 1) * QUERIES]
                for n, w in enumerate((kw, qw)):
                    if i >= 2:
                        pe.wait_ge(kq_r1, 2 * (i - 2) + n + 1)
                    nc.tensor.matmul(kq_banks(i)[n][:, :], w, xt, start=True, stop=True).then_inc(kq_made, 1)
                if i:
                    pe.wait_ge(v_kept, i)
                for q in range(QT):
                    ins = nc.tensor.matmul(scT[2][:, q * P:(q + 1) * P], xT[:, (i * QT + q) * P:(i * QT + q + 1) * P], vw,
                                           start=True, stop=True)
                ins.then_inc(v_made, 1)
                if i + 2 < SUPERS:
                    turn_x(i + 2)

            def scores_for_max(i):
                u, qt, h, c = ALL_ITEMS[i]
                s, head = super_of(u), u % GROUPS * HG + h
                if (i == ITEMS_BEFORE[u]) and u % GROUPS == 0:
                    pe.wait_ge(kq_in[s], 16 * 2 * PARTS)
                if i >= SRING:
                    pe.wait_ge(sc_used, i - SRING + 1)
                w = QUERIES if c < s else (qt + 1) * P
                nc.tensor.matmul(sc[i % SRING][:, 0:w], qT[s % 2][0:MROW, head, qt * P:(qt + 1) * P],
                                 kT[0:MROW, head, c * QUERIES:c * QUERIES + w], start=True, stop=True).then_inc(sc_made, 1)

            def turn_max(u, bank):
                pe.wait_ge(max_done, u + 1)
                for q in range(QT):
                    ins = nc.tensor.transpose(bank.bitcast(BF16)[0:2 * HG, q * P:(q + 1) * P],
                                              max16[u % 2][:, q, :, :].rearrange("p a h -> p (a h)"), ident16[:, :])
                return ins

            def scores(b, h):
                u, j = STEPS[b]
                s, off = super_of(u), first_query(u, j)
                if j == 0 and h == 0:
                    pe.wait_ge(max_in[u % 2], 32 * (u // 2 + 1))
                n = HG * b + h
                if n >= SRING:
                    pe.wait_ge(exp_done, n - SRING + 1)
                head = u % GROUPS * HG + h
                ins = nc.tensor.matmul(scT[n % SRING][:, 0:QUERIES - off], kT[:, head, j * P:(j + 1) * P],
                                       qT[s % 2][:, head, off:QUERIES], start=True, stop=True, skip_group_check=True)
                if is_diagonal(u, j):
                    ins = nc.tensor.matmul(scT[n % SRING][:, 0:P], ident16[:, :], later16[:, :], start=False, stop=True,
                                           skip_group_check=True)
                ins.then_inc(scT_made, 1)

            def attn_v(b):
                u, j = STEPS[b]
                off = first_query(u, j)
                pe.wait_ge(exp_done, HG * (b + 1))
                if j == 0 and u:
                    pe.wait_ge(y_kept, u)
                for h in range(HG):
                    head = u % GROUPS * HG + h
                    ins = nc.tensor.matmul(acc[32 * h:32 * h + VC, off:QUERIES], v[:, j, head, :],
                                           probs[(HG * b + h) % PRING][:, 0:QUERIES - off],
                                           start=(j == 0), stop=(j == unit_steps(u) - 1), skip_group_check=True)
                ins.then_inc(pv_done, 1)

            pe.wait_ge(kq_r1, 2 * SUPERS - 2)
            pe.wait_ge(s_const, 9)
            for u in range(AHEAD):
                for i in range(ITEMS_BEFORE[u], ITEMS_BEFORE[u + 1]):
                    scores_for_max(i)
                if u:
                    pe.wait_ge(maxT_kept, u)
                else:
                    pe.wait_ge(kq_r1, 2 * SUPERS)
                turn_max(u, ms[:, :]).then_inc(w_made, 1)
            pe.wait_ge(v_kept, SUPERS)
            pe.wait_ge(s_const_v, 2)
            pe.wait_ge(maxT_kept, AHEAD)

            def task(name, arg):
                t = (name, arg)
                if name not in CONSUMER:
                    return
                take_bank(pe, t)
                bank = turn_bank(t)
                if name == "max_turn":
                    ins = turn_max(arg, bank)
                if name == "y_turn":
                    s, q = divmod(arg, QT)
                    pe.wait_ge(y_kept, GROUPS * (s + 1))
                    for g in range(GROUPS):
                        ins = nc.tensor.transpose(bank[:, g * P:(g + 1) * P], yT[g][:, q * P:(q + 1) * P], ident[:, :])
                if name == "x1_turn":
                    pe.wait_ge(x1_done, arg + 1)
                    for q in range(QT):
                        ins = nc.tensor.transpose(bank[:, q * P:(q + 1) * P], x1[:, arg * QT + q, :], ident[:, :])
                if name == "logits":
                    pe.wait_ge(empty["scalar"], emptied(TURN[("x1_turn", arg)]))
                    pe.wait_ge(s_router, 16)
                    for q in range(QT):
                        ins = nc.tensor.matmul(bank[:, q * EXPERTS:(q + 1) * EXPERTS], x1T[:, q * P:(q + 1) * P], router[:, :],
                                               start=True, stop=True)
                if name == "count":
                    pe.wait_ge(mask_done, arg + 1)
                    n = 2 * MT
                    counts = bank[:, 0:n * EXPERTS].rearrange("p (n e) -> p n e", e=EXPERTS)
                    nc.tensor.matmul(counts, tri16[:, :], mask16[:, :, :], start=True, stop=False, skip_group_check=True)
                    for i in range(n - 1):
                        ins = nc.tensor.matmul(counts[:, i + 1:n, :], ones16[:, :], mask16[:, i:i + 1, :].to_broadcast([P, n - 1 - i, EXPERTS]),
                                               start=False, stop=(i == n - 2), skip_group_check=True)
                if name == "in_turn":
                    g, part = arg
                    pe.wait_ge(ein_in, 16 * (g + 1))
                    for i in range((QT, 1)[part]):
                        ins = nc.tensor.transpose(bank[:, i * P:(i + 1) * P], ein[:, part * QT + i, :], ident[:, :])
                if name == "expert_h":
                    g, e = arg
                    pe.wait_ge(empty["scalar"], emptied(TURN[("in_turn", (g, 1))]))
                    pe.wait_ge(s_ffw, 32)
                    for f in range(FC):
                        ins = nc.tensor.matmul(bank[:, f * CAP:(f + 1) * CAP], wi[:, e, f * P:(f + 1) * P],
                                               einT[:, e * CAP:(e + 1) * CAP], start=True, stop=True)
                if name == "expert_o":
                    g, e = arg
                    pe.wait_ge(empty["scalar"], emptied(TURN[("expert_h", arg)]))
                    for f in range(FC):
                        ins = nc.tensor.matmul(bank[0:CAP, 0:C], hT[e % 2][:, f, :], wo2[:, e, f, :], start=(f == 0), stop=(f == FC - 1))
                ins.then_inc(turn_made, 1)

            for b in range(LAST + 1):
                gaps = WOVEN[b] if b < NSTEP else ((), (), (), ())
                for gap in range(4):
                    for i in gaps[gap]:
                        scores_for_max(i)
                    if b < NSTEP:
                        scores(b, gap)
                if LAG <= b < NSTEP + LAG:
                    attn_v(b - LAG)
                if b == NSTEP + LAG:
                    pe.wait_ge(exp_done, HG * NSTEP)
                for t in TASKS[b]:
                    task(*t)


NAMES = ["L0_attn_x", "L0_attn_W_dq", "L0_attn_W_uq", "L0_attn_W_dkv", "L0_attn_W_uk", "L0_attn_W_uv", "L0_attn_W_o",
         "L0_ffn_w_router", "L0_ffn_wi", "L0_ffn_wo"]


def kernel(**inputs):
    import concourse.bacc as bacc
    from concourse.bass_utils import run_bass_kernel_spmd

    nc = bacc.Bacc("TRN2", target_bir_lowering=False, num_devices=1)
    arrays, args = {}, []
    for name in NAMES:
        a = np.ascontiguousarray(inputs[name])
        if name == "L0_attn_x":
            a = a.reshape(T, C)
        arrays[f"in_{name}"] = a
        args.append(nc.dram_tensor(f"in_{name}", a.shape, mybir.dt.from_np(a.dtype), kind="ExternalInput").ap())
    out = nc.dram_tensor("out_y", (T, C), F32, kind="ExternalOutput").ap()
    program(nc, *args, out)
    r = run_bass_kernel_spmd(nc, [arrays], core_ids=[0])
    return np.asarray(r.results[0]["out_y"]).reshape(1, T, C)
```
